# Optimizing a Trainium2 kernel written in Bass

```python
import numpy as np
import jax
import jax.numpy as jnp

def _softmax(x, axis=-1):
    return jax.nn.softmax(x, axis=axis)

def _gelu(x):
    return jax.nn.gelu(x, approximate=True)

def _silu(x):
    return jax.nn.silu(x)

def _sigmoid(x):
    return jax.nn.sigmoid(x)

def _layernorm(x, axis=-1, eps=1e-05):
    m = jnp.mean(x, axis=axis, keepdims=True)
    v = jnp.var(x, axis=axis, keepdims=True)
    return (x - m) / jnp.sqrt(v + eps)

def _scatter_add(tgt, idx, src, axis=0):
    return tgt.at[idx].add(src)

def _segment_sum(src, seg, n):
    return jax.ops.segment_sum(src, seg, n)
kernel_name = 'mk_decoder_postln_d2_seqx_r4_aad51a'

def setup_inputs(seed: int=0):
    np.random.seed(seed)
    _w = jnp.asarray

    def _rec_inputs():
        import jax
        import jax.numpy as jnp
        _rk = jax.random.key(seed)
        x = -0.0003929 + 0.9999 * jax.random.normal(jax.random.fold_in(_rk, 1), (2, 512, 512), jnp.float32)
        _lenS = 512 - jax.random.randint(jax.random.fold_in(_rk, 7), (2,), 0, max(1, 512 // 4) + 1, jnp.int32)
        _lenS2 = 1024 - jax.random.randint(jax.random.fold_in(_rk, 8), (2,), 0, max(1, 1024 // 4) + 1, jnp.int32)
        _ctx_1024P = jax.random.normal(jax.random.fold_in(_rk, 11), (2, 16, 256), jnp.float32)
        _ctx_1024c = jax.random.dirichlet(jax.random.fold_in(_rk, 511), 0.3 * jnp.ones((16,), jnp.float32), (2, 1024))
        _ctx_1024t = jnp.einsum('bsk,bkd->bsd', _ctx_1024c, _ctx_1024P)
        _ctx_1024t = _ctx_1024t * jax.lax.rsqrt(jnp.mean(jnp.square(_ctx_1024t)) + 1e-12) * 0.953939
        ctx_1024 = 0.000227908 + 0.99994 * (_ctx_1024t + 0.3 * jax.random.normal(jax.random.fold_in(_rk, 611), (2, 1024, 256), jnp.float32))
        _validS = jnp.arange(512)[None, :] < _lenS[:, None]
        _validS2 = jnp.arange(1024)[None, :] < _lenS2[:, None]
        _causal = jnp.tril(jnp.ones((512, 512), dtype=bool))
        mask_BxS2_bf1 = jnp.ones((2, 1024), dtype=bool)
        return (x, ctx_1024, mask_BxS2_bf1)
    x, ctx_1024, mask_BxS2_bf1 = _rec_inputs()

    def _L0_attn_setup():
        import jax, jax.numpy as jnp
        import numpy as np
        B, S, D = (2, 512, 512)
        H, HD = (16, 128)
        NEG_INF = -1e+30

        def _rope_tables(seq_len, head_dim):
            freqs = 1.0 / 10000.0 ** (np.arange(0, head_dim, 2, dtype=np.float32) / head_dim)
            pos = np.arange(seq_len, dtype=np.float32)
            ang = np.outer(pos, freqs)
            return (jnp.asarray(np.cos(ang)), jnp.asarray(np.sin(ang)))

        def _apply_rope(x, cos, sin):
            x1 = x[..., 0::2]
            x2 = x[..., 1::2]
            rx1 = x1 * cos - x2 * sin
            rx2 = x1 * sin + x2 * cos
            return jnp.stack([rx1, rx2], axis=-1).reshape(x.shape)
        key = jax.random.key(seed)
        ks = jax.random.split(key, 5)
        scale = 1.0 / np.sqrt(D)
        return {'x': jax.random.normal(ks[0], (B, S, D), dtype=jnp.float32), 'Wq': jax.random.normal(ks[1], (D, H * HD), dtype=jnp.float32) * scale, 'Wk': jax.random.normal(ks[2], (D, H * HD), dtype=jnp.float32) * scale, 'Wv': jax.random.normal(ks[3], (D, H * HD), dtype=jnp.float32) * scale, 'Wo': jax.random.normal(ks[4], (H * HD, D), dtype=jnp.float32) * scale}
    _L0_attn_all = _L0_attn_setup()
    _L0_attn_in = {k: v for k, v in _L0_attn_all.items() if k in ('Wq', 'Wk', 'Wv', 'Wo')}
    del _L0_attn_all

    def _L0_xattn_setup():
        import jax, jax.numpy as jnp
        import numpy as np
        EPS = 1e-05

        def rmsnorm(x, g, eps=EPS):
            var = jnp.mean(jnp.square(x), axis=-1, keepdims=True)
            return x * jax.lax.rsqrt(var + eps) * g
        key = jax.random.key(seed)
        ks = jax.random.split(key, 8)
        B, Sq, Skv = (2, 1024, 128)
        dim, cdim, H, D = (512, 256, 16, 128)
        inner = H * D
        s = lambda f: 1.0 / np.sqrt(f)
        return {'hidden_states': jax.random.normal(ks[0], (B, Sq, dim), jnp.float32), 'encoder_hidden_states': jax.random.normal(ks[1], (B, Skv, cdim), jnp.float32), 'Wq': jax.random.normal(ks[2], (dim, inner), jnp.float32) * s(dim), 'Wk': jax.random.normal(ks[3], (cdim, inner), jnp.float32) * s(cdim), 'Wv': jax.random.normal(ks[4], (cdim, inner), jnp.float32) * s(cdim), 'Wo': jax.random.normal(ks[5], (inner, dim), jnp.float32) * s(inner), 'gq': jnp.ones((D,), jnp.float32), 'gk': jnp.ones((D,), jnp.float32)}
    _L0_xattn_all = _L0_xattn_setup()
    _L0_xattn_in = {k: v for k, v in _L0_xattn_all.items() if k in ('Wq', 'Wk', 'Wv', 'Wo', 'gq', 'gk')}
    del _L0_xattn_all

    def _L0_ffn_setup():
        import jax, jax.numpy as jnp
        import numpy as np
        NUM_EXPERTS = 4
        key = jax.random.key(seed)
        k1, k2, k3 = jax.random.split(key, 3)
        B, N, H = (8, 512, 512)
        E = NUM_EXPERTS
        I = H * 4 // E
        x = jax.random.normal(k1, (B, N, H), dtype=jnp.float32)
        gate_up_proj = jax.random.normal(k2, (E, H, 2 * I), dtype=jnp.float32) * 0.02
        down_proj = jax.random.normal(k3, (E, I, H), dtype=jnp.float32) * 0.02
        return {'x': x, 'gate_up_proj': gate_up_proj, 'down_proj': down_proj}
    _L0_ffn_all = _L0_ffn_setup()
    _L0_ffn_in = {k: v for k, v in _L0_ffn_all.items() if k in ('gate_up_proj', 'down_proj')}
    del _L0_ffn_all

    def _L1_attn_setup():
        import jax, jax.numpy as jnp
        import numpy as np
        key = jax.random.key(seed)
        ks = jax.random.split(key, 5)
        B, S, D = (1, 1024, 512)
        H, Dh = (16, 128)
        scale = 1.0 / np.sqrt(D).astype(np.float32)
        return {'x': jax.random.normal(ks[0], (B, S, D), dtype=jnp.float32), 'W_K': jax.random.normal(ks[1], (H, Dh, D), dtype=jnp.float32) * scale, 'W_Q': jax.random.normal(ks[2], (H, Dh, D), dtype=jnp.float32) * scale, 'W_V': jax.random.normal(ks[3], (H, Dh, D), dtype=jnp.float32) * scale, 'W_O': jax.random.normal(ks[4], (D, H * Dh), dtype=jnp.float32) * scale}
    _L1_attn_all = _L1_attn_setup()
    _L1_attn_in = {k: v for k, v in _L1_attn_all.items() if k in ('W_K', 'W_Q', 'W_V', 'W_O')}
    del _L1_attn_all

    def _L1_xattn_setup():
        import jax, jax.numpy as jnp
        import numpy as np
        N_HEADS = 16
        N_KV_HEADS = 8
        HEAD_DIM = 128
        D_TEXT = 512
        D_VISION = 256
        GROUPS = N_HEADS // N_KV_HEADS
        key = jax.random.key(seed)
        ks = jax.random.split(key, 6)
        B, T_text, T_vis = (4, 512, 144)
        text_hidden = jax.random.normal(ks[0], (B, T_text, D_TEXT), dtype=jnp.float32)
        vision_tokens = jax.random.normal(ks[1], (B, T_vis, D_VISION), dtype=jnp.float32)
        vision_mask = jnp.ones((B, T_vis), dtype=bool)
        s = 0.02
        Wq = jax.random.normal(ks[2], (D_TEXT, N_HEADS * HEAD_DIM), dtype=jnp.float32) * s
        Wk = jax.random.normal(ks[3], (D_VISION, N_KV_HEADS * HEAD_DIM), dtype=jnp.float32) * s
        Wv = jax.random.normal(ks[4], (D_VISION, N_KV_HEADS * HEAD_DIM), dtype=jnp.float32) * s
        Wo = jax.random.normal(ks[5], (N_HEADS * HEAD_DIM, D_TEXT), dtype=jnp.float32) * s
        return {'text_hidden': text_hidden, 'vision_tokens': vision_tokens, 'vision_mask': vision_mask, 'Wq': Wq, 'Wk': Wk, 'Wv': Wv, 'Wo': Wo}
    _L1_xattn_all = _L1_xattn_setup()
    _L1_xattn_in = {k: v for k, v in _L1_xattn_all.items() if k in ('Wq', 'Wk', 'Wv', 'Wo')}
    del _L1_xattn_all

    def _L1_ffn_setup():
        import jax, jax.numpy as jnp
        import numpy as np
        FP8_MAX = 448.0
        GLOBAL_DIV = 448.0 * 6.0

        def _fp8(x):
            return x.astype(jnp.float8_e4m3fn).astype(jnp.float32)

        def _reorder_quantize_x(x, idx):
            scale = jnp.max(jnp.abs(x)) / GLOBAL_DIV
            xr = (x / scale)[:, idx]
            scale_x = jnp.max(jnp.abs(xr), axis=1, keepdims=True) / FP8_MAX
            qx = _fp8(xr / scale_x)
            return (qx, scale_x, scale)

        def _qlinear(qx, scale_x, scale, W, idx, out_idx=None):
            Wr = W[:, idx]
            w_scale = jnp.max(jnp.abs(Wr), axis=1, keepdims=True) / FP8_MAX
            qw = _fp8(Wr / w_scale)
            y = qx * scale_x @ (qw * w_scale).T * scale
            if out_idx is not None:
                y = y[:, out_idx]
            return y
        key = jax.random.key(seed)
        ks = jax.random.split(key, 6)
        B, S, H, I = (2, 256, 512, 1408)
        return {'x': jax.random.normal(ks[0], (B, S, H), jnp.float32), 'w_gate': jax.random.normal(ks[1], (I, H), jnp.float32) * 0.02, 'w_up': jax.random.normal(ks[2], (I, H), jnp.float32) * 0.02, 'w_down': jax.random.normal(ks[3], (H, I), jnp.float32) * 0.02, 'up_reorder_index': jax.random.permutation(ks[4], jnp.arange(H, dtype=jnp.int64)), 'down_reorder_index': jax.random.permutation(ks[5], jnp.arange(I, dtype=jnp.int64))}
    _L1_ffn_all = _L1_ffn_setup()
    _L1_ffn_in = {k: v for k, v in _L1_ffn_all.items() if k in ('w_gate', 'w_up', 'w_down', 'up_reorder_index', 'down_reorder_index')}
    del _L1_ffn_all
    return {'x': x, 'ctx_1024': ctx_1024, 'mask_BxS2_bf1': mask_BxS2_bf1, 'L0_attn_Wq': _L0_attn_in['Wq'], 'L0_attn_Wk': _L0_attn_in['Wk'], 'L0_attn_Wv': _L0_attn_in['Wv'], 'L0_attn_Wo': _L0_attn_in['Wo'], 'L0_xattn_Wq': _L0_xattn_in['Wq'], 'L0_xattn_Wk': _L0_xattn_in['Wk'], 'L0_xattn_Wv': _L0_xattn_in['Wv'], 'L0_xattn_Wo': _L0_xattn_in['Wo'], 'L0_xattn_gq': _L0_xattn_in['gq'], 'L0_xattn_gk': _L0_xattn_in['gk'], 'L0_ffn_gate_up_proj': _L0_ffn_in['gate_up_proj'], 'L0_ffn_down_proj': _L0_ffn_in['down_proj'], 'L1_attn_W_K': _L1_attn_in['W_K'], 'L1_attn_W_Q': _L1_attn_in['W_Q'], 'L1_attn_W_V': _L1_attn_in['W_V'], 'L1_attn_W_O': _L1_attn_in['W_O'], 'L1_xattn_Wq': _L1_xattn_in['Wq'], 'L1_xattn_Wk': _L1_xattn_in['Wk'], 'L1_xattn_Wv': _L1_xattn_in['Wv'], 'L1_xattn_Wo': _L1_xattn_in['Wo'], 'L1_ffn_w_gate': _L1_ffn_in['w_gate'], 'L1_ffn_w_up': _L1_ffn_in['w_up'], 'L1_ffn_w_down': _L1_ffn_in['w_down'], 'L1_ffn_up_reorder_index': _L1_ffn_in['up_reorder_index'], 'L1_ffn_down_reorder_index': _L1_ffn_in['down_reorder_index']}

def reference(x, ctx_1024, mask_BxS2_bf1, L0_attn_Wq, L0_attn_Wk, L0_attn_Wv, L0_attn_Wo, L0_xattn_Wq, L0_xattn_Wk, L0_xattn_Wv, L0_xattn_Wo, L0_xattn_gq, L0_xattn_gk, L0_ffn_gate_up_proj, L0_ffn_down_proj, L1_attn_W_K, L1_attn_W_Q, L1_attn_W_V, L1_attn_W_O, L1_xattn_Wq, L1_xattn_Wk, L1_xattn_Wv, L1_xattn_Wo, L1_ffn_w_gate, L1_ffn_w_up, L1_ffn_w_down, L1_ffn_up_reorder_index, L1_ffn_down_reorder_index):
    import jax
    import jax.numpy as jnp

    def _L0_attn_ref(x, Wq, Wk, Wv, Wo):
        import jax, jax.numpy as jnp
        import numpy as np
        B, S, D = (2, 512, 512)
        H, HD = (16, 128)
        NEG_INF = -1e+30

        def _rope_tables(seq_len, head_dim):
            freqs = 1.0 / 10000.0 ** (np.arange(0, head_dim, 2, dtype=np.float32) / head_dim)
            pos = np.arange(seq_len, dtype=np.float32)
            ang = np.outer(pos, freqs)
            return (jnp.asarray(np.cos(ang)), jnp.asarray(np.sin(ang)))

        def _apply_rope(x, cos, sin):
            x1 = x[..., 0::2]
            x2 = x[..., 1::2]
            rx1 = x1 * cos - x2 * sin
            rx2 = x1 * sin + x2 * cos
            return jnp.stack([rx1, rx2], axis=-1).reshape(x.shape)
        b, s, _ = x.shape
        cos, sin = _rope_tables(s, HD)

        def split_heads(t):
            return t.reshape(b, s, H, HD).transpose(0, 2, 1, 3)
        q = split_heads(x @ Wq)
        k = split_heads(x @ Wk)
        v = split_heads(x @ Wv)
        q = _apply_rope(q, cos, sin)
        k = _apply_rope(k, cos, sin)
        scale = 1.0 / np.sqrt(HD)
        scores = jnp.einsum('bhqd,bhkd->bhqk', q, k) * scale
        causal = jnp.triu(jnp.ones((s, s), dtype=bool), k=1)
        scores = jnp.where(causal[None, None], NEG_INF, scores)
        attn = jax.nn.softmax(scores, axis=-1)
        ctx = jnp.einsum('bhqk,bhkd->bhqd', attn, v)
        ctx = ctx.transpose(0, 2, 1, 3).reshape(b, s, H * HD)
        return ctx @ Wo

    def _L0_xattn_ref(hidden_states, encoder_hidden_states, Wq, Wk, Wv, Wo, gq, gk):
        import jax, jax.numpy as jnp
        import numpy as np
        EPS = 1e-05

        def rmsnorm(x, g, eps=EPS):
            var = jnp.mean(jnp.square(x), axis=-1, keepdims=True)
            return x * jax.lax.rsqrt(var + eps) * g
        B, Sq, _ = hidden_states.shape
        Skv = encoder_hidden_states.shape[1]
        D = gq.shape[0]
        H = Wq.shape[1] // D
        scale = 1.0 / np.sqrt(D)
        q = (hidden_states @ Wq).reshape(B, Sq, H, D)
        k = (encoder_hidden_states @ Wk).reshape(B, Skv, H, D)
        v = (encoder_hidden_states @ Wv).reshape(B, Skv, H, D)
        q = rmsnorm(q, gq)
        k = rmsnorm(k, gk)
        scores = jnp.einsum('bqhd,bkhd->bhqk', q, k) * scale
        attn = jax.nn.softmax(scores, axis=-1)
        out = jnp.einsum('bhqk,bkhd->bqhd', attn, v)
        out = out.reshape(B, Sq, H * D)
        return out @ Wo

    def _L0_ffn_ref(x, gate_up_proj, down_proj):
        import jax, jax.numpy as jnp
        import numpy as np
        NUM_EXPERTS = 4
        B, N, H = x.shape
        E, _, two_I = gate_up_proj.shape
        I = two_I // 2
        G = N // E
        x4 = x.reshape(B, G, E, H)
        gu = jnp.einsum('bgeh,ehd->bged', x4, gate_up_proj)
        gate, up = (gu[..., :I], gu[..., I:])
        inter = jax.nn.silu(gate) * up
        out = jnp.einsum('bgei,eih->bgeh', inter, down_proj)
        return out.reshape(B, N, H)

    def _L1_attn_ref(x, W_K, W_Q, W_V, W_O):
        import jax, jax.numpy as jnp
        import numpy as np
        b, pos, d_model = x.shape
        d_head = W_K.shape[1]
        k = jnp.einsum('ihd,bpd->biph', W_K, x)
        q = jnp.einsum('ihd,bpd->biph', W_Q, x)
        v = jnp.einsum('ihd,bpd->biph', W_V, x)
        scores = jnp.einsum('biph,biqh->biqp', k, q)
        mask = jnp.tril(jnp.ones((pos, pos), dtype=x.dtype))
        masked = scores * mask - jnp.float32(10000000000.0) * (1.0 - mask)
        attn = jax.nn.softmax(masked / jnp.sqrt(jnp.float32(d_head)), axis=-1)
        z = jnp.einsum('biqp,biph->biqh', attn, v)
        z_flat = jnp.transpose(z, (0, 2, 1, 3)).reshape(b, pos, -1)
        out = jnp.einsum('df,bqf->bqd', W_O, z_flat)
        return out

    def _L1_xattn_ref(text_hidden, vision_tokens, vision_mask, Wq, Wk, Wv, Wo):
        import jax, jax.numpy as jnp
        import numpy as np
        N_HEADS = 16
        N_KV_HEADS = 8
        HEAD_DIM = 128
        D_TEXT = 512
        D_VISION = 256
        GROUPS = N_HEADS // N_KV_HEADS
        B, T_text, _ = text_hidden.shape
        T_vis = vision_tokens.shape[1]
        scale = jnp.float32(np.sqrt(HEAD_DIM))
        q = (text_hidden @ Wq).reshape(B, T_text, N_HEADS, HEAD_DIM).transpose(0, 2, 1, 3)
        k = (vision_tokens @ Wk).reshape(B, T_vis, N_KV_HEADS, HEAD_DIM).transpose(0, 2, 1, 3)
        v = (vision_tokens @ Wv).reshape(B, T_vis, N_KV_HEADS, HEAD_DIM).transpose(0, 2, 1, 3)
        k = jnp.repeat(k, GROUPS, axis=1)
        v = jnp.repeat(v, GROUPS, axis=1)
        scores = jnp.einsum('bhtd,bhsd->bhts', q, k) / scale
        mask = vision_mask[:, None, None, :]
        scores = jnp.where(mask, scores, -jnp.inf)
        attn = jax.nn.softmax(scores, axis=-1)
        attn = jnp.nan_to_num(attn, nan=0.0)
        out = jnp.einsum('bhts,bhsd->bhtd', attn, v)
        out = out.transpose(0, 2, 1, 3).reshape(B, T_text, N_HEADS * HEAD_DIM)
        return out @ Wo

    def _L1_ffn_ref(x, w_gate, w_up, w_down, up_reorder_index, down_reorder_index):
        import jax, jax.numpy as jnp
        import numpy as np
        FP8_MAX = 448.0
        GLOBAL_DIV = 448.0 * 6.0

        def _fp8(x):
            return x.astype(jnp.float8_e4m3fn).astype(jnp.float32)

        def _reorder_quantize_x(x, idx):
            scale = jnp.max(jnp.abs(x)) / GLOBAL_DIV
            xr = (x / scale)[:, idx]
            scale_x = jnp.max(jnp.abs(xr), axis=1, keepdims=True) / FP8_MAX
            qx = _fp8(xr / scale_x)
            return (qx, scale_x, scale)

        def _qlinear(qx, scale_x, scale, W, idx, out_idx=None):
            Wr = W[:, idx]
            w_scale = jnp.max(jnp.abs(Wr), axis=1, keepdims=True) / FP8_MAX
            qw = _fp8(Wr / w_scale)
            y = qx * scale_x @ (qw * w_scale).T * scale
            if out_idx is not None:
                y = y[:, out_idx]
            return y
        B, S, H = x.shape
        xf = x.reshape(B * S, H)
        qx, sx, sc = _reorder_quantize_x(xf, up_reorder_index)
        g = _qlinear(qx, sx, sc, w_gate, up_reorder_index, out_idx=down_reorder_index)
        u = _qlinear(qx, sx, sc, w_up, up_reorder_index, out_idx=down_reorder_index)
        t = jax.nn.silu(g) * u
        qt, st, sct = _reorder_quantize_x(t, down_reorder_index)
        y = _qlinear(qt, st, sct, w_down, down_reorder_index)
        return y.reshape(B, S, H)
    x = _layernorm(x + _L0_attn_ref(x, L0_attn_Wq, L0_attn_Wk, L0_attn_Wv, L0_attn_Wo), axis=-1)
    x = _layernorm(x + _L0_xattn_ref(x, ctx_1024, L0_xattn_Wq, L0_xattn_Wk, L0_xattn_Wv, L0_xattn_Wo, L0_xattn_gq, L0_xattn_gk), axis=-1)
    x = _layernorm(x + _L0_ffn_ref(x, L0_ffn_gate_up_proj, L0_ffn_down_proj), axis=-1)
    x = _layernorm(x + _L1_attn_ref(x, L1_attn_W_K, L1_attn_W_Q, L1_attn_W_V, L1_attn_W_O), axis=-1)
    x = _layernorm(x + _L1_xattn_ref(x, ctx_1024, mask_BxS2_bf1, L1_xattn_Wq, L1_xattn_Wk, L1_xattn_Wv, L1_xattn_Wo), axis=-1)
    x = _layernorm(x + _L1_ffn_ref(x, L1_ffn_w_gate, L1_ffn_w_up, L1_ffn_w_down, L1_ffn_up_reorder_index, L1_ffn_down_reorder_index), axis=-1)
    return x

_drawn_inputs = setup_inputs


def setup_inputs(seed=0):
    import zlib

    import numpy as np

    out = dict(_drawn_inputs(seed))
    spreads = {'L0_xattn_gq': (1.0, 0.2), 'L0_xattn_gk': (1.0, 0.583)}
    factors = {'L1_xattn_Wq': 6.979, 'L1_xattn_Wk': 7.18}
    for name, (base, spread) in spreads.items():
        noise = np.random.default_rng([zlib.crc32(name.encode()), seed]).standard_normal(out[name].shape)
        drawn = base * np.exp(spread * noise) if base else spread * noise
        out[name] = jnp.asarray(drawn.astype(out[name].dtype))
    for name, factor in factors.items():
        out[name] = (out[name] * factor).astype(out[name].dtype)
    return out
```

```python
import numpy as np
import concourse.bass as bass
from concourse import mybir
from contextlib import ExitStack

F32, BF16, U8, I32 = mybir.dt.float32, mybir.dt.bfloat16, mybir.dt.uint8, mybir.dt.int32
ALU = mybir.AluOpType
ACT = mybir.ActivationFunctionType
AX = mybir.AxisListType

B, S, D, H, HD, SC, DC = 2, 512, 512, 16, 128, 1024, 256
P = 128
TOK = B * S
UNITS = B * H
QT = S // P
NT = TOK // P
XC, CC = D // P, DC // P
NEG = -1.0e30
EPS = 1e-5
ISQ = float(1.0 / np.sqrt(HD))
CREDIT = 8


class Layer:

    def __init__(self, name, kv, chunks, causal=False, rope=False, rms=False, gqa=False, masked=False):
        self.name, self.kv, self.chunks = name, kv, chunks
        self.causal, self.rope, self.rms, self.gqa, self.masked = causal, rope, rms, gqa, masked
        self.halves = kv // 512
        self.kt = kv // P

    def head(self, n):
        return 2 * (n // 4) + (n % 2 if self.gqa else n % 4 // 2)

    def batch(self, n):
        return n % 4 // 2 if self.gqa else n % 2

    def kvslot(self, n):
        return n // 2 % 2 if self.gqa else n % 2

    def new_kv(self, n):
        return not self.gqa or n % 2 == 0

    def jobs(self, n, qt):
        proj, pv = -1 <= n < UNITS - 1, n >= 1
        kv = self.new_kv(n + 1)
        if self.rms:
            plan = [[("K", 0)], [("KN", 0), ("K", 1)], [("KN", 1), ("Q", 0), ("PV", 0)], [("QN", 0), ("V", 0), ("V", 1)]]
        elif self.halves == 2:
            plan = [[("K", 0)], [("K", 1)], [("Q", 0), ("PV", 0)], [("V", 0), ("V", 1)]]
            if not kv:
                plan = [[("Q", 0)], [], [("PV", 0)], []]
        else:
            plan = [[("Q", 0)], [("K", 0)], [("PV", 0)], [("V", 0)]]
        return [j for j in plan[qt] if (pv if j[0] == "PV" else proj)]

    def job_list(self, n):
        return [j for qt in range(QT) for j in self.jobs(n, qt)]

    def before(self, n, qt=0, kinds=("K", "KN", "Q", "QN", "PV", "V")):
        return (sum(j[0] in kinds for m in range(-1, n) for j in self.job_list(m))
                + sum(j[0] in kinds for q in range(qt) for j in self.jobs(n, q)))


LAYERS = [Layer("self0", S, XC, causal=True, rope=True), Layer("cross0", SC, CC, rms=True),
          Layer("self1", S, XC, causal=True), Layer("cross1", SC, CC, gqa=True, masked=True)]
FFN_I, E = 512, 4
FI = 1408
IT = FI // P
STAGES = ["self0", "cross0", "ffn0", "self1", "cross1", "ffn1"]
FP8_MAX = 448.0
BY_ACT = ("K", "Q", "PV", "V")


def build(nc, a, out):
    ctx = ExitStack()
    with ctx:
        def sb(name, shape, dt, where=ctx):
            return where.enter_context(nc.sbuf_tensor(name, shape, dt))

        sem = lambda name: ctx.enter_context(nc.semaphore(name))

        xf = sb("xf", [P, NT, D], F32)
        xT = [sb(f"xT_{s}", [P, XC, TOK], BF16) for s in ("hi", "lo")]
        cT = [sb(f"cT_{s}", [P, CC, B * SC], BF16) for s in ("hi", "lo")]
        oT = [sb(f"oT_{s}", [P, H, TOK], BF16) for s in ("hi", "lo")]
        raw_q = sb("raw_q", [P, 2, 512], F32)
        raw_kv = sb("raw_kv", [P, 2, 1024], F32)
        wq = [sb(f"wq_{s}", [P, 2, XC, HD], BF16) for s in ("hi", "lo")]
        wkv = [sb(f"wkv_{s}", [P, 2, 2 * XC * HD], BF16) for s in ("hi", "lo")]
        ident = sb("ident", [P, P], F32)
        causal_bias = sb("causal_bias", [P, 512], BF16)
        stat = sb("stat", [P, NT, 6], F32)
        mv = sb("mv", [P, NT, 2], F32)
        rstd = sb("rstd", [P, NT], F32)
        half_neg = sb("half_neg", [P, QT], F32)
        ones = sb("ones", [P, P], F32)
        nb = sb("nb", [P, 2], F32)
        rs = sb("rs", [P, 2], F32)
        ri = sb("ri", [P, 2], F32)
        ps = ctx.enter_context(nc.psum_tensor("ps", [P, 8, 512], F32))
        S_BANK, T_BANK, M_BANK = 0, 4, 6

        w_in = [sem("w_in0"), sem("w_in1")]
        x_in, const_in, const_ok = sem("x_in"), sem("const_in"), sem("const_ok")
        w_split = sem("w_split")
        pool_seq, dve_seq = sem("pool_seq"), sem("dve_seq")
        job_mm, job_hi, job_lo = sem("job_mm"), sem("job_hi"), sem("job_lo")
        sq_ok, k_log, k_norm, q_norm = sem("sq_ok"), sem("k_log"), sem("k_norm"), sem("q_norm")
        rope_sum, rope_hi, rope_lo = sem("rope_sum"), sem("rope_hi"), sem("rope_lo")
        s_mm, s_max, p_exp, r_inv, p_norm = sem("s_mm"), sem("s_max"), sem("p_exp"), sem("r_inv"), sem("p_norm")
        t_mm, t_hi, t_lo = sem("t_mm"), sem("t_hi"), sem("t_lo")
        y_mm, y_add, ln_var, ln_rstd, ln_x = sem("y_mm"), sem("y_add"), sem("ln_var"), sem("ln_rstd"), sem("ln_x")
        x_mm, x_hi, x_lo = sem("x_mm"), sem("x_hi"), sem("x_lo")
        out_ok = sem("out_ok")
        row_max = sem("row_max")
        w_hi, rope_mul = sem("w_hi"), sem("rope_mul")

        gu_in, d_in, gu_hi, d_hi, gu_lo, d_lo = (sem(x) for x in ("gu_in", "d_in", "gu_hi", "d_hi", "gu_lo", "d_lo"))
        gu_mm, silu_ok, prod_ok, inter_hi, inter_lo = (sem(x) for x in ("gu_mm", "silu_ok", "prod_ok", "inter_hi", "inter_lo"))
        idx_in, row_in0, row_in1, rowd_in, row_y, q_m, q_w, q_ok, q_mm, q_T, diag_ok, diag_mm, diag_cp = (
            sem(x) for x in ("idx_in", "row_in0", "row_in1", "rowd_in", "row_y", "q_m", "q_w", "q_ok", "q_mm", "q_T", "diag_ok", "diag_mm", "diag_cp"))
        fg_mm, fu_mm, g_ok, gs_ok, fs_ok, fy_ok = (sem(x) for x in ("fg_mm", "fu_mm", "g_ok", "gs_ok", "fs_ok", "fy_ok"))
        idb_ok = sem("idb_ok")
        row_in = [row_in0, row_in1]

        by_name = {L.name: L for L in LAYERS}
        names = STAGES
        stages = [by_name.get(n) for n in names]
        ledger, c = [], dict(job=0, hi=0, lo=CREDIT, sq=0, nrm=0, rope=0, s=0, x=0, split=0, win0=0, win1=0, ln=0, seq=0)
        for L in stages:
            if L is None:
                ledger.append(dict(c))
                c["ln"] += NT
                continue
            if L.name == "cross0":
                c["split"] += 4; c["win0"] += 32; c["win1"] += 32
            ledger.append(dict(c))
            c["job"] += L.before(UNITS + 1)
            c["hi"] += L.before(UNITS + 1, kinds=BY_ACT)
            c["lo"] += L.before(UNITS + 1)
            if L.rms:
                c["sq"] += L.before(UNITS + 1, kinds=("K", "Q"))
                c["nrm"] += L.before(UNITS + 1, kinds=("KN", "QN"))
            if L.rope:
                c["rope"] += L.before(UNITS + 1, kinds=("K", "Q"))
            c["s"] += UNITS * QT
            c["x"] += UNITS * QT * L.halves
            c["split"] += 2 * H
            c["win0"] += 16 * (2 * H // 2) + 16 * (H // 2)
            c["win1"] += 16 * ((1 if L.gqa else 2) * H // 2) + 16 * (H // 2)
            c["ln"] += NT

        def units(engine, unit):
            unit(0, None)
            with engine.Fori(0, 7) as it:
                for i in range(4):
                    unit(1 + i, it)
            for n in range(UNITS - 3, UNITS):
                unit(n, None)

        def at(f, n, it):
            return f(n) if it is None else it * (f(n + 4) - f(n)) + f(n)

        scope = []
        mem = []
        for li, L in enumerate(stages):
            s = ExitStack()
            m = {}
            hl = ("hi", "lo")
            if names[li] == "ffn0":
                m["raw_gu"] = sb("raw_gu", [P, XC, 2 * FFN_I], F32, s)
                m["raw_d"] = sb("raw_d", [P, FFN_I // P, D], F32, s)
                m["gu"] = [sb(f"gu_{k}", [P, 2, XC, 2 * FFN_I], BF16, s) for k in hl]
                m["d"] = [sb(f"d_{k}", [P, 2, FFN_I // P, D], BF16, s) for k in hl]
                m["sg"] = sb("sg", [P, 4, TOK // E], F32, s)
                m["pr"] = sb("pr", [P, 4, TOK // E], F32, s)
                m["in"] = [oT[k][:, 0:2, :].rearrange("p s (i n) -> p s i n", n=TOK // E) for k in range(2)]
            if names[li] == "ffn1":
                m["idx"] = sb("idx", [P, IT], I32, s)
                m["row"] = sb("row", [P, 2, FI], F32, s)
                m["M"] = sb("M", [P, 2, FI], F32, s)
                m["Q"] = sb("Q", [P, 2, FI], BF16, s)
                m["SG"] = sb("SG", [P, 2, FI], F32, s)
                m["sB"] = sb("sB", [P, 2 * FI + D], F32, s)
                m["diag"] = sb("diag", [P, 2, P], F32, s)
                m["mx"] = sb("mxq", [P, 64], F32, s)
                m["r"] = sb("rq", [P, 64], F32, s)
                m["sc"] = sb("scq", [P, 64], F32, s)
                m["qxT"] = sb("qxT", [P, 2, XC, P], BF16, s)
                m["qtT"] = sb("qtT", [P, 2, IT, P], BF16, s)
                m["idb"] = sb("idb", [P, P], BF16, s)
                m["yt"] = sb("yt", [P, D], F32, s)
                flat0 = oT[0][:, :, :].rearrange("p h n -> p (h n)")
                flat1 = oT[1][:, :, :].rearrange("p h n -> p (h n)")
                m["wT"] = flat0[:, 0:2 * XC * FI].rearrange("p (c i) -> p c i", i=FI)
                m["wdT"] = flat1[:, 0:IT * D].rearrange("p (c i) -> p c i", i=D)
            if L is None:
                s.close()
                mem.append(m)
                continue
            m["q"] = [sb(f"q{li}_{k}", [P, 2, S], BF16, s) for k in hl]
            m["k"] = [sb(f"k{li}_{k}", [P, 2, L.kv], BF16, s) for k in hl]
            m["v"] = [sb(f"v{li}_{k}", [P, 2, L.kt, HD], BF16, s) for k in hl]
            m["p"] = sb(f"p{li}", [P, 2, L.kv], F32, s)
            m["pT"] = [sb(f"pT{li}_{k}", [P, 2, 8, S], BF16, s) for k in hl]
            if L.rope:
                m["cos"], m["sin"] = sb("cos", [P, S], F32, s), sb("sin", [P, S], F32, s)
                m["rot"], m["swap"] = sb("rot", [P, 2, S], F32, s), sb("swap", [P, 2, S], F32, s)
            if L.rms:
                m["sq"] = sb("sq", [P, S], F32, s)
                m["rk"] = sb("rk", [P, 2, SC], F32, s)
                m["nq"] = sb("nq", [P, 2, QT], F32, s)
                m["g"] = sb("g", [P, 2], F32, s)
                m["mx"] = sb("mx", [P, 2], F32, s)
                m["gg"] = sb("gg", [P, 1], F32, s)
            if L.masked:
                m["m8"] = sb("m8", [P, B, SC], U8, s)
                m["mb"] = sb("mb", [P, B, SC], BF16, s)
                m["any"] = sb("any", [P, B], F32, s)
            s.close()
            mem.append(m)

        def tiles(name):
            if name == "ffn0":
                return [(4 * b + e, 4 + 2 * (e % 2) + b) for e in range(E) for b in range(B)]
            if name == "ffn1":
                return [(t, 7) for t in range(NT)]
            return [(t, t) for t in range(NT)]

        WJ = [("g", t) for t in range(IT)] + [("u", t) for t in range(IT)] + [("d", t) for t in range(D // P)]
        QJ = WJ + [("x", 0)]
        for t in range(NT):
            QJ += ([("x", t + 1)] if t + 1 < NT else []) + [("t", t)]
        QN = {j: k for k, j in enumerate(QJ)}
        width = lambda kind: FI if kind in ("d", "t") else D
        CH = [(0, 512), (512, 1024), (1024, FI)]

        block = ctx.enter_context(nc.Block())

        @block.sync
        def _(sp):
            sp.dma_start(xf[:, :, :], a["x"].rearrange("b (p e) d -> p b e d", e=4)).then_inc(x_in, 16)
            for li, L in enumerate(stages):
                if names[li] == "ffn0":
                    m = mem[li]
                    sp.wait_ge(job_mm, ledger[li]["job"])
                    for e in range(E):
                        if e:
                            sp.wait_ge(gu_lo, e)
                        sp.dma_start(m["raw_gu"][:, :, :], a["gu"][e]).then_inc(gu_in, 16)
                        if e:
                            sp.wait_ge(d_lo, e)
                        sp.dma_start(m["raw_d"][:, :, :], a["down"][e]).then_inc(d_in, 16)
                    continue
                if names[li] == "ffn1":
                    m = mem[li]
                    sp.wait_ge(ln_x, NT * li)
                    sp.dma_start(m["idx"][:, :], a["didx"]).then_inc(idx_in, 16)
                    for t in range(D // P):
                        k = QN[("d", t)]
                        sp.wait_ge(q_ok, k - 1)
                        sp.dma_start(m["row"][:, k % 2, :], a["wdown"][t * P:(t + 1) * P, :]).then_inc(rowd_in, 16)
                        sp.wait_ge(rowd_in, 16 * (t + 1))
                    continue
                c, base = ledger[li], ledger[li]["split"]
                if L.rope:
                    sp.dma_start(mem[li]["cos"][:, :], a["cos"]).then_inc(const_in, 16)
                    sp.dma_start(mem[li]["sin"][:, :], a["sin"]).then_inc(const_in, 16)
                if L.name == "cross0":
                    for k in range(4):
                        sp.wait_ge(w_split, base - 4 + k - 1)
                        sp.dma_start(raw_kv[:, k % 2, :], a["ctxT"][:, k, :]).then_inc(w_in[k % 2], 16)
                cols = 2 * L.chunks * HD

                def qkv(g, j, free):
                    if free is not None:
                        sp.wait_ge(w_split, free)
                    sp.dma_start(raw_q[:, j, :], a["wq" + L.name][bass.ds(2 * g + j, 1), :, :].rearrange("o p n -> p (o n)")).then_inc(w_in[j], 16)
                    if not L.gqa:
                        sp.dma_start(raw_kv[:, j, 0:cols], a["wkv" + L.name][bass.ds(2 * g + j, 1), :, :].rearrange("o p n -> p (o n)")).then_inc(w_in[j], 16)
                    elif j == 0:
                        sp.dma_start(raw_kv[:, j, 0:cols], a["wkv" + L.name][bass.ds(g, 1), :, :].rearrange("o p n -> p (o n)")).then_inc(w_in[j], 16)

                for j in range(2):
                    qkv(0, j, None if li == 0 else base + j - 1)
                if L.rms:
                    sp.wait_ge(ln_x, NT * li)
                    sp.dma_start(mem[li]["g"][:, :], a["gqk"]).then_inc(const_in, 16)
                if L.masked:
                    sp.wait_ge(ln_x, NT * li)
                    sp.dma_start(mem[li]["m8"][:, :, :], a["mask"].partition_broadcast(P)).then_inc(const_in, 16)
                with sp.Fori(1, H // 2) as g:
                    for j in range(2):
                        qkv(g, j, g * 2 + (base + j - 1))
                with sp.Fori(0, H // 2) as g:
                    for j in range(2):
                        sp.wait_ge(w_split, g * 2 + (base + H + j - 1))
                        sp.dma_start(raw_q[:, j, :], a["wo" + L.name][bass.ds(2 * g + j, 1), :, :].rearrange("o p n -> p (o n)")).then_inc(w_in[j], 16)
            sp.wait_ge(ln_x, NT * len(stages))
            sp.dma_start(out.rearrange("b (p e) d -> p b e d", e=4), xf[:, :, :]).then_inc(out_ok, 16)
            sp.wait_ge(out_ok, 16)

        @block.gpsimd
        def _(pool):
            nseq = [0]

            def own(ins):
                nseq[0] += 1
                ins.then_inc(pool_seq, 1)
                pool.wait_ge(pool_seq, nseq[0])

            own(nc.gpsimd.memset(ident[:, :], 0.0))
            nc.gpsimd.affine_select(out=ident[:, :], in_=ident[:, :], compare_op=ALU.not_equal, fill=1.0,
                                    base=0, pattern=[[-1, P]], channel_multiplier=1).then_inc(const_ok, 1)
            own(nc.gpsimd.memset(causal_bias[:, :], 0.0))
            nc.gpsimd.affine_select(out=causal_bias[:, :], in_=causal_bias[:, :], compare_op=ALU.is_ge, fill=NEG,
                                    base=384, pattern=[[-1, 512]], channel_multiplier=1).then_inc(const_ok, 1)
            nc.gpsimd.memset(half_neg[:, :], -0.5).then_inc(const_ok, 1)
            nc.gpsimd.memset(ones[:, :], 1.0).then_inc(const_ok, 1)
            pool.wait_ge(const_ok, 4)

            def split_item(pairs, waits, item):
                for s, v in waits:
                    pool.wait_ge(s, v)
                pool.nop(nofuse=True)
                for dst, src in pairs:
                    last = nc.gpsimd.tensor_scalar(dst[0], src, 1.0, 1.0, ALU.mult, ALU.mult)
                last.then_inc(w_hi, 1)
                pool.wait_ge(w_hi, item)
                for dst, src in pairs:
                    last = nc.gpsimd.tensor_tensor(dst[1], src, dst[0], ALU.subtract)
                last.then_inc(w_split, 1)

            def qkv_splitter(li):
                L = stages[li]
                cols = 2 * L.chunks * HD

                def split_qkv(j, value, used, item):
                    pairs = [((wq[0][:, j, :, :].rearrange("p c d -> p (c d)"), wq[1][:, j, :, :].rearrange("p c d -> p (c d)")), raw_q[:, j, :])]
                    if not L.gqa or j == 0:
                        pairs.append(((wkv[0][:, j, 0:cols], wkv[1][:, j, 0:cols]), raw_kv[:, j, 0:cols]))
                    split_item(pairs, [(w_in[j], value)] + ([(job_mm, used)] if used is not None else []), item)
                return split_qkv

            def start_layer(li):
                L, c, m = stages[li], ledger[li], mem[li]
                if L.name == "cross0":
                    for k in range(4):
                        half, chunk = k // 2, k % 2
                        sl = slice(half * SC, (half + 1) * SC)
                        split_item([((cT[0][:, chunk, sl], cT[1][:, chunk, sl]), raw_kv[:, k % 2, :])],
                                   [(w_in[k % 2], c[f"win{k % 2}"] - 32 + 16 * (k // 2 + 1))], c["split"] - 4 + k + 1)
                split_qkv = qkv_splitter(li)
                for j in range(2):
                    split_qkv(j, c[f"win{j}"] + (32 if j == 0 or not L.gqa else 16), c["job"] if li else None, c["split"] + j + 1)

            for li, L in enumerate(stages):
                c, m = ledger[li], mem[li]

                def inv_std(k):
                    t = tiles(names[li])[k][0]
                    pool.wait_ge(ln_var, c["ln"] + k + 1)
                    own(nc.gpsimd.tensor_scalar(rstd[:, t:t + 1], mv[:, t, 1:2], EPS, None, ALU.add))
                    nc.gpsimd.tensor_tensor(rstd[:, t:t + 1], rstd[:, t:t + 1], half_neg[:, 0:1], ALU.pow).then_inc(ln_rstd, 1)

                if L is not None and L.rms:
                    pool.wait_ge(const_in, 48)
                    nc.gpsimd.tensor_tensor(m["gg"][:, :], m["g"][:, 0:1], m["g"][:, 1:2], ALU.mult).then_inc(const_ok, 1)
                if L is not None and L.masked:
                    pool.wait_ge(const_in, 64)
                    nc.gpsimd.tensor_scalar(m["mb"][:, :, :], m["m8"][:, :, :], -NEG, NEG, ALU.mult, ALU.add).then_inc(const_ok, 1)

                if names[li] == "ffn0":
                    def gu_low(e):
                        pool.wait_ge(gu_hi, e + 1)
                        nc.gpsimd.tensor_tensor(m["gu"][1][:, e % 2, :, :], m["raw_gu"][:, :, :], m["gu"][0][:, e % 2, :, :], ALU.subtract).then_inc(gu_lo, 1)
                    gu_low(0)
                    gu_low(1)
                    for e in range(E + 1):
                        if e == E:
                            start_layer(li + 1)
                        if e:
                            inv_std(2 * e - 2)
                            inv_std(2 * e - 1)
                        if e + 2 < E:
                            gu_low(e + 2)
                    continue
                if names[li] == "ffn1":
                    pool.wait_ge(idx_in, 16)
                    nc.gpsimd.tensor_scalar(m["idb"][:, :], ident[:, :], 1.0, 1.0, ALU.mult, ALU.mult).then_inc(idb_ok, 1)

                    def gather(k):
                        kind, t = QJ[k]
                        nc.gpsimd.indirect_dma_start(out=m["row"][:, k % 2, 0:D], out_offset=None, in_=a["wgate" if kind == "g" else "wup"],
                                                     in_offset=bass.IndirectOffsetOnAxis(ap=m["idx"][:, t:t + 1].bitcast(mybir.dt.uint32), axis=0)).then_inc(row_in[k % 2], 16)

                    gather(0)
                    gather(1)
                    for k, (kind, t) in enumerate(QJ):
                        w = width(kind)
                        y, M = m["row"][:, k % 2, 0:w], m["M"][:, k % 2, 0:w]
                        if kind == "t":
                            for u in ([0, 1] if t == 0 else [t + 1] if t + 1 < NT else []):
                                pool.wait_ge(fs_ok, u + 1)
                                nc.gpsimd.tensor_tensor(m["SG"][:, u % 2, :], m["SG"][:, u % 2, :], m["sB"][:, FI:2 * FI], ALU.mult).then_inc(gs_ok, 1)
                        pool.wait_ge(q_m, k + 1)
                        nc.gpsimd.tensor_tensor(y, y, M, ALU.add).then_inc(q_w, 1)
                        if k >= 2:
                            pool.wait_ge(q_mm, k - 1)
                        pool.wait_ge(q_w, k + 1)
                        nc.gpsimd.tensor_tensor(m["Q"][:, k % 2, 0:w], y, M, ALU.subtract).then_inc(q_ok, 1)
                        if k + 2 < 2 * IT:
                            pool.wait_ge(q_ok, k + 1)
                            gather(k + 2)
                        if kind == "t" and t:
                            inv_std(t - 1)
                    inv_std(NT - 1)
                    continue
                cols = 2 * L.chunks * HD
                pT = m["pT"]

                if not li:
                    start_layer(li)
                split_qkv = qkv_splitter(li)
                def query_norms(n, it, qt, jobs):
                    for x, (kind, _) in enumerate(jobs):
                        if kind == "QN":
                            pool.wait_ge(job_lo, at(lambda n: c["lo"] + L.before(n, qt) + x + 1, n, it))
                            r = m["nq"][:, (n + 1) % 2, :]
                            nc.gpsimd.tensor_tensor(r, r, half_neg[:, 0:QT], ALU.pow).then_inc(q_norm, 1)

                def rope(n, it, qt, jobs):
                    for x, (kind, _) in enumerate(jobs):
                        if kind not in ("K", "Q"):
                            continue
                        r = ("Q", "K").index(kind)
                        hi = lambda n: c["hi"] + L.before(n, qt, BY_ACT) + x + 1
                        lo = lambda n: c["lo"] + L.before(n, qt) + x + 1
                        pool.wait_ge(job_hi, at(hi, n, it))
                        nc.gpsimd.tensor_tensor(m["swap"][:, r, :], m["swap"][:, r, :], m["sin"][:, :], ALU.mult).then_inc(rope_mul, 1)
                        pool.wait_ge(rope_mul, at(lambda n: c["rope"] + 2 * (n + 1) + r + 1, n, it))
                        pool.wait_ge(job_lo, at(lo, n, it))
                        nc.gpsimd.tensor_tensor(m["rot"][:, r, :], m["rot"][:, r, :], m["swap"][:, r, :], ALU.add).then_inc(rope_sum, 1)

                def unit(n, it):
                    if n % 4 >= 2 and n // 4 < H // 2 - 1:
                        j = n % 4 - 2
                        value = lambda n: c[f"win{j}"] + (32 if j == 0 or not L.gqa else 16) * (n // 4 + 2)
                        split_qkv(j, at(value, n, it), at(lambda n: c["job"] + L.before(n), n, it),
                                  at(lambda n: c["split"] + 2 * (n // 4) + 2 + j + 1, n, it))
                    for qt in range(QT):
                        w = P * (qt + 1) if L.causal else L.kv
                        s = lambda n: c["s"] + QT * n + qt + 1
                        pool.wait_ge(r_inv, at(s, n, it))
                        pool.nop(nofuse=True)
                        nc.gpsimd.tensor_scalar(m["p"][:, qt % 2, 0:w], m["p"][:, qt % 2, 0:w], ri[:, qt % 2:qt % 2 + 1], 1.0,
                                                ALU.mult, ALU.mult).then_inc(p_norm, 1)
                        if L.rope:
                            rope(n, it, qt, L.jobs(n, qt))
                        if L.rms:
                            query_norms(n, it, qt, L.jobs(n, qt))

                for qt in range(QT):
                    if L.rope:
                        rope(-1, None, qt, L.jobs(-1, qt))
                    if L.rms:
                        query_norms(-1, None, qt, L.jobs(-1, qt))
                units(pool, unit)

                for slot in range(2):
                    n_pv = c["job"] + (L.before(UNITS) if slot == 0 else L.before(UNITS + 1))
                    pool.wait_ge(job_mm, n_pv)
                    for k in range(8):
                        h, j = 8 * slot + k, k % 2
                        win = c[f"win{j}"] + 16 * (H // 2) * (1 if L.gqa and j == 1 else 2) + 16 * (h // 2 + 1)
                        split_item([((pT[0][:, slot, k, :], pT[1][:, slot, k, :]), raw_q[:, j, :])], [(w_in[j], win)], c["split"] + H + h + 1)

                if li + 1 < len(stages) and stages[li + 1] is not None:
                    start_layer(li + 1)
                for t in range(NT):
                    inv_std(t)

        @block.scalar
        def _(act):
            def x_part(n, t, bank):
                act.wait_ge(x_mm, n + 1)
                b, e = t // 4, t % 4
                nc.scalar.activation(xT[0][:, :, b * S + e:(b + 1) * S:4], ps[:, bank, :].rearrange("p (c n) -> p c n", c=XC), ACT.Copy).then_inc(x_hi, 1)

            nc.scalar.preload_act_table_set("natural_log_exp_and_others")
            for t in range(NT):
                x_part(t, t, t)
            for li, L in enumerate(stages):
                c, m = ledger[li], mem[li]
                if L is not None and li:
                    nc.scalar.preload_act_table_set("natural_log_exp_and_others")
                if names[li] == "ffn0":
                    def weights_hi(e):
                        if e >= 2:
                            act.wait_ge(y_mm, c["ln"] + 2 * (e - 1))
                        act.wait_ge(gu_in, 16 * (e + 1))
                        nc.scalar.activation(m["gu"][0][:, e % 2, :, :], m["raw_gu"][:, :, :], ACT.Copy).then_inc(gu_hi, 1)
                        act.wait_ge(d_in, 16 * (e + 1))
                        nc.scalar.activation(m["d"][0][:, e % 2, :, :], m["raw_d"][:, :, :], ACT.Copy).then_inc(d_hi, 1)

                    weights_hi(0)
                    weights_hi(1)
                    for e in range(E + 2):
                        if e < E:
                            for i in range(4):
                                act.wait_ge(gu_mm, 4 * e + i + 1)
                                if e:
                                    act.wait_ge(prod_ok, 4 * (e - 1) + i + 1)
                                nc.scalar.activation(m["sg"][:, i, :], ps[:, i, 0:TOK // E], ACT.Silu).then_inc(silu_ok, 1)
                            act.wait_ge(prod_ok, 4 * (e + 1))
                            nc.scalar.activation(m["in"][0][:, e % 2, :, :], m["pr"][:, :, :], ACT.Copy).then_inc(inter_hi, 1)
                        if e >= 2:
                            for k in (2 * e - 4, 2 * e - 3):
                                x_part(NT + c["ln"] + k, *tiles("ffn0")[k])
                        if e + 2 < E:
                            weights_hi(e + 2)
                    continue
                if names[li] == "ffn1":
                    for k, (kind, t) in enumerate(QJ):
                        if kind == "t":
                            for u in ([0, 1] if t == 0 else [t + 1] if t + 1 < NT else []):
                                act.wait_ge(g_ok, u + 1)
                                sx = m["sc"][:, QN[("x", u)]:QN[("x", u)] + 1]
                                nc.scalar.activation(m["SG"][:, u % 2, :], m["SG"][:, u % 2, :], ACT.Silu, scale=sx).then_inc(fs_ok, 1)
                        act.wait_ge(q_mm, k + 1)
                        lo = ps[:, 6, :].bitcast(BF16).rearrange("p (c n) -> p c n", n=P)
                        hi = ps[:, 7, :].bitcast(BF16).rearrange("p (c n) -> p c n", n=P)
                        if kind in "gu":
                            o = XC if kind == "u" else 0
                            nc.scalar.activation(m["wT"][:, o:o + XC, t * P:(t + 1) * P], lo[:, 0:XC, :], ACT.Copy).then_inc(q_T, 1)
                        elif kind == "x":
                            nc.scalar.activation(m["qxT"][:, t % 2, :, :], lo[:, 0:XC, :], ACT.Copy).then_inc(q_T, 1)
                        else:
                            dst = m["wdT"][:, :, t * P:(t + 1) * P] if kind == "d" else m["qtT"][:, t % 2, :, :]
                            nc.scalar.activation(dst[:, 0:8, :], lo[:, :, :], ACT.Copy)
                            nc.scalar.activation(dst[:, 8:IT, :], hi[:, 0:IT - 8, :], ACT.Copy).then_inc(q_T, 1)
                        if kind in "gud":
                            act.wait_ge(diag_mm, k + 1)
                            o = {"g": 0, "u": FI, "d": 2 * FI}[kind] + t * P
                            nc.scalar.activation(m["sB"][:, o:o + P], ps[:, 5, 0:P], ACT.Copy).then_inc(diag_cp, 1)
                    continue

                def job_parts(n, it, qt, jobs):
                    b, u = L.batch(n + 1), n + 1
                    for x, (kind, half) in enumerate(jobs):
                        if kind not in BY_ACT:
                            continue
                        bank = ps[:, M_BANK + (L.before(n, qt) + x) % 2, :]
                        act.wait_ge(job_mm, at(lambda n: c["job"] + L.before(n, qt) + x + 1, n, it))
                        if kind == "PV":
                            h = at(L.head, n - 1, it)
                            pb = L.batch(n - 1)
                            o = oT[0][:, bass.ds(h, 1), pb * S:(pb + 1) * S]
                            src = bank.rearrange("p (o n) -> p o n", o=1)
                            if L.masked:
                                nc.scalar.activation(o, src, ACT.Copy, scale=m["any"][:, pb:pb + 1]).then_inc(job_hi, 1)
                            else:
                                nc.scalar.activation(o, src, ACT.Copy).then_inc(job_hi, 1)
                        elif kind == "V":
                            nc.scalar.activation(m["v"][0][:, L.kvslot(u), 4 * half:4 * half + 4, :], bank.rearrange("p (t d) -> p t d", d=HD), ACT.Copy).then_inc(job_hi, 1)
                        elif L.rope:
                            r = ("Q", "K").index(kind)
                            nc.scalar.activation(m["swap"][0:64, r, :], bank[64:128, :], ACT.Copy)
                            nc.scalar.activation(m["swap"][64:128, r, :], bank[0:64, :], ACT.Copy).then_inc(job_hi, 1)
                        else:
                            if L.rms:
                                nc.scalar.activation(m["sq"][:, :], bank, ACT.Square).then_inc(sq_ok, 1)
                            if kind == "Q":
                                nc.scalar.activation(m["q"][0][:, u % 2, :], bank, ACT.Copy).then_inc(job_hi, 1)
                            else:
                                o = m["k"][0][:, L.kvslot(u), half * 512:half * 512 + 512]
                                if L.rms:
                                    nc.scalar.activation(o, bank, ACT.Copy, scale=m["gg"][:, 0:1]).then_inc(job_hi, 1)
                                else:
                                    nc.scalar.activation(o, bank, ACT.Copy).then_inc(job_hi, 1)

                def key_norms(n, it, qt, jobs):
                    for x, (kind, half) in enumerate(jobs):
                        if (kind, half) == ("KN", 1):
                            act.wait_ge(job_lo, at(lambda n: c["lo"] + L.before(n, qt) + x + 1, n, it))
                            r = m["rk"][:, (n + 1) % 2, :]
                            nc.scalar.activation(r, r, ACT.Ln).then_inc(k_log, 1)
                            act.wait_ge(k_log, at(lambda n: n + 2, n, it))
                            nc.scalar.activation(r, r, ACT.Exp, scale=-0.5).then_inc(k_norm, 1)

                def rotated(n, it, qt, jobs):
                    for kind, _ in jobs:
                        if kind in ("K", "Q"):
                            r = ("Q", "K").index(kind)
                            act.wait_ge(rope_sum, at(lambda n: c["rope"] + 2 * (n + 1) + r + 1, n, it))
                            nc.scalar.activation(m[kind.lower()][0][:, (n + 1) % 2, :], m["rot"][:, r, :], ACT.Copy).then_inc(rope_hi, 1)

                def turned(n, it, qt):
                    for half in range(L.halves):
                        blocks = qt + 1 if L.causal else 4
                        idx = lambda n: c["x"] + (QT * n + qt) * L.halves + half
                        act.wait_ge(t_mm, at(lambda n: idx(n) + 1, n, it))
                        bank = ps[:, T_BANK + idx(n) % 2, 0:blocks * P].rearrange("p (k q) -> p k q", q=P)
                        nc.scalar.activation(m["pT"][0][:, n % 2, 4 * half:4 * half + blocks, qt * P:qt * P + P], bank, ACT.Copy).then_inc(t_hi, 1)

                def unit(n, it):
                    for qt in range(QT):
                        w = P * (qt + 1) if L.causal else L.kv
                        act.wait_ge(s_max, at(lambda n: CREDIT + c["s"] + QT * n + qt + 1, n, it))
                        prob = m["p"][:, qt % 2, 0:w]
                        nc.scalar.activation(prob, prob, ACT.Exp, scale=1.0 if L.rms else -1.0, bias=nb[:, qt % 2:qt % 2 + 1], accum_out=rs[:, qt % 2:qt % 2 + 1]).then_inc(p_exp, 1)
                        job_parts(n, it, qt, L.jobs(n, qt))
                        if L.rope and qt > 0:
                            rotated(n, it, qt - 1, L.jobs(n, qt - 1))
                        if qt > 0:
                            turned(n, it, qt - 1)
                        elif n > 0:
                            turned(n - 1, it, QT - 1)
                        if L.rms:
                            key_norms(n, it, qt, L.jobs(n, qt))

                if L.rms:
                    act.wait_ge(const_ok, 5)
                if L.masked:
                    act.wait_ge(const_ok, 7)
                for qt in range(QT):
                    job_parts(-1, None, qt, L.jobs(-1, qt))
                    if L.rope:
                        rotated(-1, None, qt, L.jobs(-1, qt))
                    if L.rms:
                        key_norms(-1, None, qt, L.jobs(-1, qt))
                units(act, unit)
                turned(UNITS - 1, None, QT - 1)
                for qt in range(QT):
                    job_parts(UNITS, None, qt, L.jobs(UNITS, qt))
                for t in range(NT):
                    x_part(NT * (li + 1) + t, t, t)

        @block.vector
        def _(dve):
            nseq = [0]

            def own(ins):
                nseq[0] += 1
                ins.then_inc(dve_seq, 1)
                dve.wait_ge(dve_seq, nseq[0])

            dve.sem_inc(job_lo, CREDIT)
            dve.sem_inc(s_max, CREDIT)
            dve.sem_inc(t_lo, CREDIT)

            def x_part(n, t, bank):
                dve.wait_ge(x_hi, n + 1)
                b, e = t // 4, t % 4
                sl = slice(b * S + e, (b + 1) * S, 4)
                nc.vector.tensor_tensor(xT[1][:, :, sl], ps[:, bank, :].rearrange("p (c n) -> p c n", c=XC), xT[0][:, :, sl], ALU.subtract).then_inc(x_lo, 1)

            for t in range(NT):
                x_part(t, t, t)
            for li, L in enumerate(stages):
                c, m = ledger[li], mem[li]

                def residual(k):
                    t, bank = tiles(names[li])[k]
                    dve.wait_ge(y_mm, c["ln"] + k + 1)
                    if names[li] == "ffn1":
                        n = QN[("t", t)]
                        ins = nc.vector.scalar_tensor_tensor(out=m["yt"][:, :], in0=ps[:, bank, :], scalar=m["sc"][:, n:n + 1], in1=m["sB"][:, 2 * FI:2 * FI + D],
                                                             op0=ALU.mult, op1=ALU.mult)
                        ins.then_inc(fy_ok, 1)
                        dve.wait_ge(fy_ok, k + 1)
                        own(nc.vector.tensor_tensor(xf[:, t, :], m["yt"][:, :], xf[:, t, :], ALU.add))
                    else:
                        own(nc.vector.tensor_tensor(xf[:, t, :], ps[:, bank, :], xf[:, t, :], ALU.add))
                    own(nc.vector.bn_stats(stat[:, t, :], xf[:, t, :]))
                    nc.vector.bn_aggr(mv[:, t, :], stat[:, t, :]).then_inc(ln_var, 1)

                def normalise(k):
                    t = tiles(names[li])[k][0]
                    dve.wait_ge(ln_rstd, c["ln"] + k + 1)
                    dve.wait_ge(ln_var, c["ln"] + k + 1)
                    nc.vector.tensor_scalar(xf[:, t, :], xf[:, t, :], mv[:, t, 0:1], rstd[:, t:t + 1], ALU.subtract, ALU.mult).then_inc(ln_x, 1)

                if names[li] == "ffn0":
                    def down_low(e):
                        dve.wait_ge(d_hi, e + 1)
                        nc.vector.tensor_tensor(m["d"][1][:, e % 2, :, :], m["raw_d"][:, :, :], m["d"][0][:, e % 2, :, :], ALU.subtract).then_inc(d_lo, 1)
                    down_low(0)
                    down_low(1)
                    for e in range(E + 2):
                        if e < E:
                            for i in range(4):
                                dve.wait_ge(silu_ok, 4 * e + i + 1)
                                if e:
                                    dve.wait_ge(inter_hi, e)
                                    dve.wait_ge(inter_lo, e)
                                nc.vector.tensor_tensor(m["pr"][:, i, :], ps[:, i, TOK // E:2 * TOK // E], m["sg"][:, i, :], ALU.mult).then_inc(prod_ok, 1)
                            dve.wait_ge(inter_hi, e + 1)
                            nc.vector.tensor_tensor(m["in"][1][:, e % 2, :, :], m["pr"][:, :, :], m["in"][0][:, e % 2, :, :], ALU.subtract).then_inc(inter_lo, 1)
                        if e >= 2:
                            for k in (2 * e - 4, 2 * e - 3):
                                x_part(NT + c["ln"] + k, *tiles("ffn0")[k])
                        if 1 <= e <= E:
                            residual(2 * e - 2)
                            residual(2 * e - 1)
                            normalise(2 * e - 2)
                            normalise(2 * e - 1)
                        if e + 2 < E:
                            down_low(e + 2)
                    continue
                if names[li] == "ffn1":
                    for k, (kind, t) in enumerate(QJ):
                        w = width(kind)
                        y, M, col = m["row"][:, k % 2, 0:w], m["M"][:, k % 2, 0:w], slice(k, k + 1)
                        if k >= 2:
                            dve.wait_ge(q_ok, k - 1)
                        if kind in "gu":
                            dve.wait_ge(row_in[k % 2], 16 * (k // 2 + 1))
                        elif kind == "d":
                            dve.wait_ge(rowd_in, 16 * (t + 1))
                        elif kind == "t":
                            if t == 0:
                                dve.wait_ge(diag_cp, len(WJ))
                            for u in ([0, 1] if t == 0 else [t + 1] if t + 1 < NT else []):
                                dve.wait_ge(fg_mm, u + 1)
                                if u >= 2:
                                    dve.wait_ge(row_y, u - 1)
                                nc.vector.tensor_tensor(m["SG"][:, u % 2, :], ps[:, 0:3, :].rearrange("p a n -> p (a n)")[:, 0:FI], m["sB"][:, 0:FI], ALU.mult).then_inc(g_ok, 1)
                            dve.wait_ge(fu_mm, t + 1)
                            dve.wait_ge(gs_ok, t + 1)
                            sx = m["sc"][:, QN[("x", t)]:QN[("x", t)] + 1]
                            nc.vector.scalar_tensor_tensor(out=y, in0=ps[:, 3:6, :].rearrange("p a n -> p (a n)")[:, 0:FI], scalar=sx, in1=m["SG"][:, t % 2, :], op0=ALU.mult, op1=ALU.mult).then_inc(row_y, 1)
                            dve.wait_ge(row_y, t + 1)
                        src = xf[:, t, :] if kind == "x" else y
                        own(nc.vector.tensor_reduce(m["mx"][:, col], src, AX.X, ALU.max, apply_absolute_value=True))
                        nc.vector.tensor_scalar(m["sc"][:, col], m["mx"][:, col], 1.0 / FP8_MAX, None, ALU.mult)
                        own(nc.vector.reciprocal(m["r"][:, col], m["mx"][:, col]))
                        own(nc.vector.tensor_scalar(y, src, m["r"][:, col], FP8_MAX, ALU.mult, ALU.mult))
                        own(nc.vector.tensor_scalar(M.bitcast(I32), y.bitcast(I32), 0x7F800000, None, ALU.bitwise_and))
                        nc.vector.tensor_scalar(M, M, 2.0 ** -6, 1.5 * 2.0 ** 20, ALU.max, ALU.mult).then_inc(q_m, 1)
                        if kind in "gud":
                            if k >= 2:
                                dve.wait_ge(diag_mm, k - 1)
                            nc.vector.tensor_scalar(m["diag"][:, k % 2, :], ident[:, :], m["sc"][:, col], None, ALU.mult).then_inc(diag_ok, 1)
                        if kind == "t" and t:
                            residual(t - 1)
                            normalise(t - 1)
                    residual(NT - 1)
                    normalise(NT - 1)
                    continue

                def job_parts(n, it, qt, jobs):
                    u = n + 1
                    for x, (kind, half) in enumerate(jobs):
                        bank = ps[:, M_BANK + (L.before(n, qt) + x) % 2, :]
                        acts = sum(k in BY_ACT for k, _ in jobs[:x + 1])
                        if kind in BY_ACT:
                            dve.wait_ge(job_hi, at(lambda n: c["hi"] + L.before(n, qt, BY_ACT) + acts, n, it))
                        else:
                            dve.wait_ge(job_mm, at(lambda n: c["job"] + L.before(n, qt) + x + 1, n, it))
                        if kind == "PV":
                            h = at(L.head, n - 1, it)
                            pb = L.batch(n - 1)
                            o, hi = (oT[k][:, bass.ds(h, 1), pb * S:(pb + 1) * S] for k in (1, 0))
                            src = bank.rearrange("p (o n) -> p o n", o=1)
                            if L.masked:
                                nc.vector.scalar_tensor_tensor(out=o, in0=src, scalar=m["any"][:, pb:pb + 1], in1=hi, op0=ALU.mult, op1=ALU.subtract).then_inc(job_lo, 1)
                            else:
                                nc.vector.tensor_tensor(o, src, hi, ALU.subtract).then_inc(job_lo, 1)
                        elif kind == "V":
                            o, hi = (m["v"][k][:, L.kvslot(u), 4 * half:4 * half + 4, :] for k in (1, 0))
                            nc.vector.tensor_tensor(o, bank.rearrange("p (t d) -> p t d", d=HD), hi, ALU.subtract).then_inc(job_lo, 1)
                        elif kind == "KN":
                            nc.vector.tensor_scalar(m["rk"][:, u % 2, half * 512:half * 512 + 512], bank, 1.0 / HD, EPS, ALU.mult, ALU.add).then_inc(job_lo, 1)
                        elif kind == "QN":
                            nc.vector.tensor_scalar(m["nq"][:, u % 2, :], bank[:, 0:QT], 1.0, EPS * HD, ALU.mult, ALU.add).then_inc(job_lo, 1)
                        elif L.rope:
                            r = ("Q", "K").index(kind)
                            nc.vector.tensor_tensor(m["rot"][:, r, :], bank, m["cos"][:, :], ALU.mult).then_inc(job_lo, 1)
                        elif kind == "Q":
                            nc.vector.tensor_tensor(m["q"][1][:, u % 2, :], bank, m["q"][0][:, u % 2, :], ALU.subtract).then_inc(job_lo, 1)
                        else:
                            o, hi = (m["k"][k][:, L.kvslot(u), half * 512:half * 512 + 512] for k in (1, 0))
                            if L.rms:
                                nc.vector.scalar_tensor_tensor(out=o, in0=bank, scalar=m["gg"][:, 0:1], in1=hi, op0=ALU.mult, op1=ALU.subtract).then_inc(job_lo, 1)
                            else:
                                nc.vector.tensor_tensor(o, bank, hi, ALU.subtract).then_inc(job_lo, 1)

                def rotated(n, it, qt, jobs):
                    for kind, _ in jobs:
                        if kind in ("K", "Q"):
                            r = ("Q", "K").index(kind)
                            dve.wait_ge(rope_hi, at(lambda n: c["rope"] + 2 * (n + 1) + r + 1, n, it))
                            o, hi = (m[kind.lower()][k][:, (n + 1) % 2, :] for k in (1, 0))
                            nc.vector.tensor_tensor(o, m["rot"][:, r, :], hi, ALU.subtract).then_inc(rope_lo, 1)

                def turned(n, it, qt):
                    for half in range(L.halves):
                        blocks = qt + 1 if L.causal else 4
                        idx = lambda n: c["x"] + (QT * n + qt) * L.halves + half
                        dve.wait_ge(t_hi, at(lambda n: idx(n) + 1, n, it))
                        bank = ps[:, T_BANK + idx(n) % 2, 0:blocks * P].rearrange("p (k q) -> p k q", q=P)
                        o, hi = (m["pT"][k][:, n % 2, 4 * half:4 * half + blocks, qt * P:qt * P + P] for k in (1, 0))
                        nc.vector.tensor_tensor(o, bank, hi, ALU.subtract).then_inc(t_lo, 1)

                def scores(n, it, qt):
                    w = P * (qt + 1) if L.causal else L.kv
                    dve.wait_ge(s_mm, at(lambda n: c["s"] + QT * n + qt + 1, n, it))
                    dve.nop(nofuse=True)
                    bank = ps[:, S_BANK + 2 * (qt % 2):S_BANK + 2 * (qt % 2) + L.halves, :].rearrange("p a n -> p (a n)")[:, 0:w]
                    kw = dict(out=m["p"][:, qt % 2, 0:w], in0=bank, scalar=3.0e38, op1=ALU.min, accum_out=nb[:, qt % 2:qt % 2 + 1])
                    if L.causal:
                        ins = nc.vector.tensor_tensor_reduce(in1=causal_bias[:, 512 - w:512], scale=-ISQ, op0=ALU.add, **kw)
                    elif L.masked:
                        ins = nc.vector.tensor_tensor_reduce(in1=m["mb"][:, L.batch(n), :], scale=-ISQ, op0=ALU.add, **kw)
                    else:
                        if qt == 0:
                            dve.wait_ge(k_norm, at(lambda n: n + 1, n, it))
                            dve.wait_ge(q_norm, at(lambda n: n + 1, n, it))
                            dve.nop(nofuse=True)
                        kw.update(scalar=-3.0e38, op1=ALU.max, accum_out=m["mx"][:, qt % 2:qt % 2 + 1])
                        nc.vector.tensor_tensor_reduce(in1=m["rk"][:, n % 2, :], scale=m["nq"][:, n % 2, qt:qt + 1], op0=ALU.mult, **kw).then_inc(row_max, 1)
                        dve.wait_ge(row_max, at(lambda n: QT * n + qt + 1, n, it))
                        ins = nc.vector.tensor_scalar(nb[:, qt % 2:qt % 2 + 1], m["mx"][:, qt % 2:qt % 2 + 1], -1.0, None, ALU.mult)
                    ins.then_inc(s_max, 1)

                def unit(n, it):
                    for qt in range(QT):
                        scores(n, it, qt)
                        dve.wait_ge(p_exp, at(lambda n: c["s"] + QT * n + qt + 1, n, it))
                        nc.vector.reciprocal(ri[:, qt % 2:qt % 2 + 1], rs[:, qt % 2:qt % 2 + 1]).then_inc(r_inv, 1)
                        job_parts(n, it, qt, L.jobs(n, qt))
                        if L.rope and qt > 0:
                            rotated(n, it, qt - 1, L.jobs(n, qt - 1))
                        if qt > 0:
                            turned(n, it, qt - 1)
                        elif n > 0:
                            turned(n - 1, it, QT - 1)

                if L.rope:
                    dve.wait_ge(const_in, 32)
                    dve.wait_ge(const_ok, 2)
                if L.rms:
                    dve.wait_ge(const_ok, 5)
                if L.masked:
                    dve.wait_ge(const_in, 64)
                    nc.vector.tensor_reduce(m["any"][:, :], m["m8"][:, :, :], AX.X, ALU.max).then_inc(const_ok, 1)
                    dve.wait_ge(const_ok, 7)
                for qt in range(QT):
                    job_parts(-1, None, qt, L.jobs(-1, qt))
                    if L.rope:
                        rotated(-1, None, qt, L.jobs(-1, qt))
                units(dve, unit)
                turned(UNITS - 1, None, QT - 1)
                for qt in range(QT):
                    job_parts(UNITS, None, qt, L.jobs(UNITS, qt))

                for k in range(NT + 3):
                    if k < NT:
                        residual(k)
                    if 0 <= k - 1 < NT:
                        normalise(k - 1)
                    if 0 <= k - 3 < NT:
                        x_part(NT * (li + 1) + k - 3, k - 3, k - 3)

        @block.tensor
        def _(pe):
            def three(o, l, r, first, last):
                nc.tensor.matmul(o, l(0), r(0), start=first, stop=False)
                nc.tensor.matmul(o, l(0), r(1), start=False, stop=False)
                return nc.tensor.matmul(o, l(1), r(0), start=False, stop=last)

            def turn_x(t, bank):
                for ch in range(XC):
                    last = nc.tensor.transpose(ps[:, bank, ch * P:ch * P + P], xf[:, t, ch * P:ch * P + P], ident[:, :])
                last.then_inc(x_mm, 1)

            pe.wait_ge(const_ok, 4)
            pe.wait_ge(x_in, 16)
            for t in range(NT):
                turn_x(t, t)
            for li, L in enumerate(stages):
                c, m = ledger[li], mem[li]
                if names[li] == "ffn0":
                    pe.wait_ge(x_lo, c["ln"] + NT)
                    n = TOK // E
                    for e in range(E + 2):
                        if e < E:
                            pe.wait_ge(gu_lo, e + 1)
                            for i in range(4):
                                if e:
                                    pe.wait_ge(prod_ok, 4 * (e - 1) + i + 1)
                                for part in range(2):
                                    for ch in range(XC):
                                        o = part * FFN_I + i * P
                                        last = three(ps[:, i, part * n:part * n + n], lambda k: m["gu"][k][:, e % 2, ch, o:o + P],
                                                     lambda k: xT[k][:, ch, e:TOK:E], ch == 0, ch == XC - 1)
                                last.then_inc(gu_mm, 1)
                        if e >= 2:
                            for k in (2 * e - 4, 2 * e - 3):
                                pe.wait_ge(ln_x, c["ln"] + k + 1)
                                turn_x(*tiles("ffn0")[k])
                        if 1 <= e <= E:
                            pe.wait_ge(inter_lo, e)
                            pe.wait_ge(d_lo, e)
                            if e >= 3:
                                pe.wait_ge(x_lo, NT + c["ln"] + 2 * (e - 2))
                            for b in range(B):
                                bank = tiles("ffn0")[2 * e - 2 + b][1]
                                for i in range(4):
                                    last = three(ps[:, bank, :], lambda k: m["in"][k][:, (e - 1) % 2, i, b * P:b * P + P], lambda k: m["d"][k][:, (e - 1) % 2, i, :], i == 0, i == 3)
                                last.then_inc(y_mm, 1)
                    continue
                if names[li] == "ffn1":
                    def turn_q(k):
                        kind, t = QJ[k]
                        pe.wait_ge(q_ok, k + 1)
                        if k:
                            pe.wait_ge(q_T, k)
                        if kind == "t" and t:
                            pe.wait_ge(fy_ok, t)
                        for blk in range(width(kind) // P):
                            bank = ps[:, 6 + blk // 8, :].bitcast(BF16)
                            last = nc.tensor.transpose(bank[:, blk % 8 * P:blk % 8 * P + P], m["Q"][:, k % 2, blk * P:blk * P + P], m["idb"][:, :])
                        last.then_inc(q_mm, 1)
                        if kind in "gud":
                            pe.wait_ge(diag_ok, k + 1)
                            if k:
                                pe.wait_ge(diag_cp, k)
                            nc.tensor.matmul(ps[:, 5, 0:P], ones[:, :], m["diag"][:, k % 2, :], start=True, stop=True).then_inc(diag_mm, 1)

                    pe.wait_ge(idb_ok, 1)
                    pe.wait_ge(x_lo, c["ln"] + NT)
                    for k in range(len(WJ)):
                        turn_q(k)
                    pe.wait_ge(diag_cp, len(WJ))

                    def up(t):
                        turn_q(QN[("x", t)])
                        pe.wait_ge(q_T, QN[("x", t)] + 1)
                        for part, done in ((0, fg_mm), (1, fu_mm)):
                            if t:
                                pe.wait_ge(row_y if part else g_ok, t)
                            for n, (lo, hi) in enumerate(CH):
                                for ch in range(XC):
                                    last = nc.tensor.matmul(ps[:, 3 * part + n, 0:hi - lo], m["qxT"][:, t % 2, ch, :], m["wT"][:, part * XC + ch, lo:hi], start=ch == 0, stop=ch == XC - 1)
                            last.then_inc(done, 1)

                    up(0)
                    up(1)
                    for t in range(NT):
                        turn_q(QN[("t", t)])
                        pe.wait_ge(q_T, QN[("t", t)] + 1)
                        for i in range(IT):
                            last = nc.tensor.matmul(ps[:, 7, :], m["qtT"][:, t % 2, i, :], m["wdT"][:, i, :], start=i == 0, stop=i == IT - 1)
                        last.then_inc(y_mm, 1)
                        if t + 2 < NT:
                            up(t + 2)
                    continue
                src = xT if L.chunks == XC else cT

                def job(n, it, qt, x, kind, half):
                    b, u = L.batch(n + 1), n + 1
                    bank = ps[:, M_BANK + (L.before(n, qt) + x) % 2, :]
                    pe.wait_ge(job_lo, at(lambda n: c["lo"] + L.before(n, qt) + x - 1, n, it))
                    if kind in ("Q", "K", "V"):
                        pe.wait_ge(w_split, at(lambda n: c["split"] + L.head(n + 1) + 1, n, it))
                    j = L.head(u) % 2
                    w = lambda part, seg, ch: wkv[part][:, j if not L.gqa else 0, (seg * L.chunks + ch) * HD:(seg * L.chunks + ch + 1) * HD]
                    span = S if L.chunks == XC else SC
                    if kind == "Q":
                        for ch in range(XC):
                            last = three(bank, lambda k: wq[k][:, j, ch, :], lambda k: xT[k][:, ch, b * S:(b + 1) * S], ch == 0, ch == XC - 1)
                    elif kind == "K":
                        o = b * span + half * 512
                        for ch in range(L.chunks):
                            last = three(bank, lambda k: w(k, 0, ch), lambda k: src[k][:, ch, o:o + 512], ch == 0, ch == L.chunks - 1)
                    elif kind == "V":
                        for t in range(4):
                            o = b * span + half * 512 + t * P
                            for ch in range(L.chunks):
                                last = three(bank[:, t * P:t * P + P], lambda k: src[k][:, ch, o:o + P], lambda k: w(k, 1, ch), ch == 0, ch == L.chunks - 1)
                    elif kind == "KN":
                        pe.wait_ge(sq_ok, at(lambda n: c["sq"] + 3 * (n + 1) + half + 1, n, it))
                        last = nc.tensor.matmul(bank, ones[:, :], m["sq"][:, :], start=True, stop=True)
                    elif kind == "QN":
                        pe.wait_ge(sq_ok, at(lambda n: c["sq"] + 3 * (n + 1) + 3, n, it))
                        for q in range(QT):
                            last = nc.tensor.matmul(bank[:, q:q + 1], m["sq"][:, q * P:q * P + P], ones[:, 0:1], start=True, stop=True)
                    else:
                        v, pT = L.kvslot(n - 1), (n - 1) % 2
                        pe.wait_ge(t_lo, at(lambda n: CREDIT + c["x"] + QT * n * L.halves, n, it))
                        for kt in range(L.kt):
                            q0 = kt * P if L.causal else 0
                            last = three(bank[:, q0:S], lambda k: m["v"][k][:, v, kt, :], lambda k: m["pT"][k][:, pT, kt, q0:S], kt == 0, kt == L.kt - 1)
                    last.then_inc(job_mm, 1)

                def turn(n, it, qt):
                    pe.wait_ge(p_norm, at(lambda n: c["s"] + QT * n + qt + 1, n, it))
                    for half in range(L.halves):
                        idx = lambda n: c["x"] + (QT * n + qt) * L.halves + half
                        pe.wait_ge(t_lo, at(lambda n: CREDIT + idx(n) - 1, n, it))
                        for k in range(qt + 1 if L.causal else 4):
                            kk = (4 * half + k) * P
                            last = nc.tensor.transpose(ps[:, T_BANK + idx(n) % 2, k * P:k * P + P], m["p"][:, qt % 2, kk:kk + P], ident[:, :])
                        last.then_inc(t_mm, 1)

                def unit(n, it):
                    for qt in range(QT):
                        if qt == 0:
                            pe.wait_ge(job_lo, at(lambda n: c["lo"] + L.before(n - 1, QT - 1), n, it))
                            if L.rope:
                                pe.wait_ge(rope_lo, at(lambda n: c["rope"] + 2 * (n + 1), n, it))
                        pe.wait_ge(s_max, at(lambda n: CREDIT + c["s"] + QT * n + qt - 1, n, it))
                        for half in range(L.halves):
                            w = P * (qt + 1) if L.causal else 512
                            last = three(ps[:, S_BANK + 2 * (qt % 2) + half, 0:w], lambda k: m["q"][k][:, n % 2, qt * P:qt * P + P],
                                         lambda k: m["k"][k][:, L.kvslot(n), half * 512:half * 512 + w], True, True)
                        last.then_inc(s_mm, 1)
                        for x, (kind, half) in enumerate(L.jobs(n, qt)):
                            job(n, it, qt, x, kind, half)
                        if qt > 0:
                            turn(n, it, qt - 1)
                        elif n > 0:
                            turn(n - 1, it, QT - 1)

                pe.wait_ge(x_lo, c["ln"] + NT)
                for qt in range(QT):
                    for x, (kind, half) in enumerate(L.jobs(-1, qt)):
                        job(-1, None, qt, x, kind, half)
                units(pe, unit)
                turn(UNITS - 1, None, QT - 1)
                for qt in range(QT):
                    for x, (kind, half) in enumerate(L.jobs(UNITS, qt)):
                        job(UNITS, None, qt, x, kind, half)

                pe.wait_ge(job_lo, c["lo"] + L.before(UNITS + 1))
                def project(t, h, first, last):
                    b, e = t // 4, t % 4
                    cols = slice(b * S + e, (b + 1) * S, 4)
                    return three(ps[:, t, :], lambda k: oT[k][:, h, cols], lambda k: m["pT"][k][:, h // 8, h % 8, :], first, last)
                for h in range(8):
                    pe.wait_ge(w_split, c["split"] + H + h + 1)
                    for t in range(NT):
                        project(t, h, h == 0, False)
                pe.wait_ge(w_split, c["split"] + 2 * H)
                for t in range(NT + 2):
                    if t < NT:
                        for h in range(8, H):
                            last = project(t, h, False, h == H - 1)
                        last.then_inc(y_mm, 1)
                    if t >= 2:
                        pe.wait_ge(ln_x, c["ln"] + t - 1)
                        turn_x(t - 2, t - 2)


def kernel(**inputs):
    import numpy as _np
    import concourse.bacc as _bacc
    from concourse import mybir as _mybir
    from concourse.bass_utils import run_bass_kernel_spmd as _run

    def heads(w, chunks, perm=None):
        w = _np.asarray(w).reshape(chunks, P, -1, HD)
        if perm is not None:
            w = w[..., perm]
        return w.transpose(2, 1, 0, 3)

    def kv(k, v):
        k = _np.concatenate([k, v], axis=2)
        return k.reshape(k.shape[0], P, -1)

    flat = lambda q: q.reshape(q.shape[0], P, -1)
    i = {k: _np.asarray(v) for k, v in inputs.items()}
    perm = _np.concatenate([_np.arange(0, HD, 2), _np.arange(1, HD, 2)])
    freq = 1.0 / 10000.0 ** (_np.arange(0, HD, 2, dtype=_np.float32) / HD)
    ang = _np.outer(freq, _np.arange(S, dtype=_np.float32)).astype(_np.float32)
    arrays = {
        "x": i["x"],
        "ctxT": i["ctx_1024"].reshape(B, SC, CC, P).transpose(3, 0, 2, 1).reshape(P, B * CC, SC),
        "gqk": _np.stack([i["L0_xattn_gq"], i["L0_xattn_gk"]], axis=1),
        "cos": _np.concatenate([_np.cos(ang), _np.cos(ang)]),
        "sin": _np.concatenate([-_np.sin(ang), _np.sin(ang)]),
        "mask": i["mask_BxS2_bf1"].view(_np.uint8),
        "wqself0": flat(heads(i["L0_attn_Wq"], XC, perm)),
        "wkvself0": kv(heads(i["L0_attn_Wk"], XC, perm), heads(i["L0_attn_Wv"], XC)),
        "woself0": i["L0_attn_Wo"].reshape(H, P, D),
        "wqcross0": flat(heads(i["L0_xattn_Wq"], XC)),
        "wkvcross0": kv(heads(i["L0_xattn_Wk"], CC), heads(i["L0_xattn_Wv"], CC)),
        "wocross0": i["L0_xattn_Wo"].reshape(H, P, D),
        "wqself1": flat(heads(i["L1_attn_W_Q"].reshape(H * HD, D).T, XC)),
        "wkvself1": kv(heads(i["L1_attn_W_K"].reshape(H * HD, D).T, XC), heads(i["L1_attn_W_V"].reshape(H * HD, D).T, XC)),
        "woself1": i["L1_attn_W_O"].T.reshape(H, P, D),
        "wqcross1": flat(heads(i["L1_xattn_Wq"], XC)),
        "wkvcross1": kv(heads(i["L1_xattn_Wk"], CC), heads(i["L1_xattn_Wv"], CC)),
        "wocross1": i["L1_xattn_Wo"].reshape(H, P, D),
    }
    arrays["gu"] = i["L0_ffn_gate_up_proj"].reshape(E, XC, P, 2 * FFN_I).transpose(0, 2, 1, 3)
    arrays["down"] = i["L0_ffn_down_proj"].reshape(E, FFN_I // P, P, D).transpose(0, 2, 1, 3)
    arrays["wgate"], arrays["wup"], arrays["wdown"] = i["L1_ffn_w_gate"], i["L1_ffn_w_up"], i["L1_ffn_w_down"]
    arrays["didx"] = i["L1_ffn_down_reorder_index"].reshape(IT, P).T
    nc = _bacc.Bacc("TRN2", target_bir_lowering=False, num_devices=1, dynamic_dma_scratch_size=4096)
    arrays = {f"in_{k}": _np.ascontiguousarray(v) for k, v in arrays.items()}
    args = {k[3:]: nc.dram_tensor(k, v.shape, _mybir.dt.from_np(v.dtype), kind="ExternalInput").ap() for k, v in arrays.items()}
    o = nc.dram_tensor("out_0", (B, S, D), _mybir.dt.float32, kind="ExternalOutput").ap()
    build(nc, args, o)
    r = _run(nc, [arrays], core_ids=[0])
    return r.results[0]["out_0"]
```

```python
import numpy as np
import concourse.bass as bass
from concourse import mybir
from contextlib import ExitStack

F32, BF16, U8, I32 = mybir.dt.float32, mybir.dt.bfloat16, mybir.dt.uint8, mybir.dt.int32
ALU = mybir.AluOpType
ACT = mybir.ActivationFunctionType
AX = mybir.AxisListType

B, S, D, H, HD, SC, DC = 2, 512, 512, 16, 128, 1024, 256
P = 128
TOK = B * S
UNITS = B * H
QT = S // P
NT = TOK // P
XC, CC = D // P, DC // P
NEG = -1.0e30
EPS = 1e-5
ISQ = float(1.0 / np.sqrt(HD))
CREDIT = 8


class Layer:

    def __init__(self, name, kv, chunks, causal=False, rope=False, rms=False, gqa=False, masked=False):
        self.name, self.kv, self.chunks = name, kv, chunks
        self.causal, self.rope, self.rms, self.gqa, self.masked = causal, rope, rms, gqa, masked
        self.halves = kv // 512
        self.kt = kv // P

    def head(self, n):
        return 2 * (n // 4) + (n % 2 if self.gqa else n % 4 // 2)

    def batch(self, n):
        return n % 4 // 2 if self.gqa else n % 2

    def kvslot(self, n):
        return n // 2 % 2 if self.gqa else n % 2

    def new_kv(self, n):
        return not self.gqa or n % 2 == 0

    def jobs(self, n, qt):
        proj, pv = -1 <= n < UNITS - 1, n >= 1
        kv = self.new_kv(n + 1)
        if self.rms:
            plan = [[("K", 0)], [("KN", 0), ("K", 1)], [("KN", 1), ("Q", 0), ("PV", 0)], [("QN", 0), ("V", 0), ("V", 1)]]
        elif self.halves == 2:
            plan = [[("K", 0)], [("K", 1)], [("Q", 0), ("PV", 0)], [("V", 0), ("V", 1)]]
            if not kv:
                plan = [[("Q", 0)], [], [("PV", 0)], []]
        else:
            plan = [[("Q", 0)], [("K", 0)], [("PV", 0)], [("V", 0)]]
        return [j for j in plan[qt] if (pv if j[0] == "PV" else proj)]

    def job_list(self, n):
        return [j for qt in range(QT) for j in self.jobs(n, qt)]

    def before(self, n, qt=0, kinds=("K", "KN", "Q", "QN", "PV", "V")):
        return (sum(j[0] in kinds for m in range(-1, n) for j in self.job_list(m))
                + sum(j[0] in kinds for q in range(qt) for j in self.jobs(n, q)))


LAYERS = [Layer("self0", S, XC, causal=True, rope=True), Layer("cross0", SC, CC, rms=True),
          Layer("self1", S, XC, causal=True), Layer("cross1", SC, CC, gqa=True, masked=True)]
FFN_I, E = 512, 4
FI = 1408
IT = FI // P
STAGES = ["self0", "cross0", "ffn0", "self1", "cross1", "ffn1"]
FP8_MAX = 448.0
BY_ACT = ("K", "Q", "PV", "V")


def build(nc, a, out):
    ctx = ExitStack()
    with ctx:
        def sb(name, shape, dt, where=ctx):
            return where.enter_context(nc.sbuf_tensor(name, shape, dt))

        sem = lambda name: ctx.enter_context(nc.semaphore(name))

        xf = sb("xf", [P, NT, D], F32)
        xT = [sb(f"xT_{s}", [P, XC, TOK], BF16) for s in ("hi", "lo")]
        cT = [sb(f"cT_{s}", [P, CC, B * SC], BF16) for s in ("hi", "lo")]
        oT = [sb(f"oT_{s}", [P, H, TOK], BF16) for s in ("hi", "lo")]
        raw_q = sb("raw_q", [P, 2, 512], F32)
        raw_kv = sb("raw_kv", [P, 2, 1024], F32)
        wq = [sb(f"wq_{s}", [P, 2, XC, HD], BF16) for s in ("hi", "lo")]
        wkv = [sb(f"wkv_{s}", [P, 2, 2 * XC * HD], BF16) for s in ("hi", "lo")]
        ident = sb("ident", [P, P], F32)
        idb = sb("idb", [P, P], BF16)
        causal_bias = sb("causal_bias", [P, 512], BF16)
        stat = sb("stat", [P, NT, 6], F32)
        mv = sb("mv", [P, NT, 2], F32)
        rstd = sb("rstd", [P, NT], F32)
        half_neg = sb("half_neg", [P, QT], F32)
        ones = sb("ones", [P, P], F32)
        idx = sb("idx", [P, IT], I32)
        q_max, q_inv, q_scale = (sb(x, [P, 48], F32) for x in ("q_max", "q_inv", "q_scale"))
        nb = sb("nb", [P, 2], F32)
        rs = sb("rs", [P, 2], F32)
        ri = sb("ri", [P, 2], F32)
        ps = ctx.enter_context(nc.psum_tensor("ps", [P, 8, 512], F32))
        S_BANK, T_BANK, M_BANK = 0, 4, 6

        w_in = [sem("w_in0"), sem("w_in1")]
        x_in, const_in, const_ok = sem("x_in"), sem("const_in"), sem("const_ok")
        w_split = sem("w_split")
        pool_seq, dve_seq = sem("pool_seq"), sem("dve_seq")
        job_mm, job_hi, job_lo = sem("job_mm"), sem("job_hi"), sem("job_lo")
        sq_ok, k_log, k_norm, q_norm = sem("sq_ok"), sem("k_log"), sem("k_norm"), sem("q_norm")
        rope_sum, rope_hi, rope_lo = sem("rope_sum"), sem("rope_hi"), sem("rope_lo")
        s_mm, s_max, p_exp, r_inv, p_norm = sem("s_mm"), sem("s_max"), sem("p_exp"), sem("r_inv"), sem("p_norm")
        t_mm, t_hi, t_lo = sem("t_mm"), sem("t_hi"), sem("t_lo")
        y_mm, y_add, ln_var, ln_rstd, ln_x = sem("y_mm"), sem("y_add"), sem("ln_var"), sem("ln_rstd"), sem("ln_x")
        x_mm, x_hi, x_lo = sem("x_mm"), sem("x_hi"), sem("x_lo")
        out_ok = sem("out_ok")
        row_max = sem("row_max")
        w_hi, rope_mul = sem("w_hi"), sem("rope_mul")

        gu_in, d_in = [sem("gu_in0"), sem("gu_in1")], [sem("d_in0"), sem("d_in1")]
        gu_hi, d_hi, gate_lo, up_lo, d_lo = (sem(x) for x in ("gu_hi", "d_hi", "gate_lo", "up_lo", "d_lo"))
        gu_mm, silu_ok, prod_ok, inter_hi, inter_lo = (sem(x) for x in ("gu_mm", "silu_ok", "prod_ok", "inter_hi", "inter_lo"))
        idx_in, rowd_in, row_y, q_m, q_w, q_ok, q_mm, q_T, diag_ok, diag_mm, diag_cp = (
            sem(x) for x in ("idx_in", "rowd_in", "row_y", "q_m", "q_w", "q_ok", "q_mm", "q_T", "diag_ok", "diag_mm", "diag_cp"))
        fg_mm, fu_mm, g_ok, gs_ok, fs_ok, fy_ok = (sem(x) for x in ("fg_mm", "fu_mm", "g_ok", "gs_ok", "fs_ok", "fy_ok"))
        idb_ok, q_a, q_s = sem("idb_ok"), sem("q_a"), sem("q_s")
        row_in = [sem(f"row_in{i}") for i in range(4)]

        by_name = {L.name: L for L in LAYERS}
        names = STAGES
        stages = [by_name.get(n) for n in names]
        ledger, c = [], dict(job=0, hi=0, lo=CREDIT, sq=0, nrm=0, rope=0, s=0, x=0, split=0, win0=0, win1=0, ln=0, seq=0)
        for L in stages:
            if L is None:
                ledger.append(dict(c))
                c["ln"] += NT
                continue
            if L.name == "cross0":
                c["split"] += 4; c["win0"] += 32; c["win1"] += 32
            ledger.append(dict(c))
            c["job"] += L.before(UNITS + 1)
            c["hi"] += L.before(UNITS + 1, kinds=BY_ACT)
            c["lo"] += L.before(UNITS + 1)
            if L.rms:
                c["sq"] += L.before(UNITS + 1, kinds=("K", "Q"))
                c["nrm"] += L.before(UNITS + 1, kinds=("KN", "QN"))
            if L.rope:
                c["rope"] += L.before(UNITS + 1, kinds=("K", "Q"))
            c["s"] += UNITS * QT
            c["x"] += UNITS * QT * L.halves
            c["split"] += 2 * H
            c["win0"] += 16 * (2 * H // 2) + 16 * (H // 2)
            c["win1"] += 16 * ((1 if L.gqa else 2) * H // 2) + 16 * (H // 2)
            c["ln"] += NT

        def units(engine, unit):
            unit(0, None)
            with engine.Fori(0, 7) as it:
                for i in range(4):
                    unit(1 + i, it)
            for n in range(UNITS - 3, UNITS):
                unit(n, None)

        def at(f, n, it):
            return f(n) if it is None else it * (f(n + 4) - f(n)) + f(n)

        mem = []
        for li, L in enumerate(stages):
            s = ExitStack()
            m = {}
            hl = ("hi", "lo")
            if names[li] == "ffn0":
                spare = [t[:, 2:, :].rearrange("p h n -> p (h n)").bitcast(F32) for t in oT]
                m["raw_gu"] = [sb("raw_gu", [P, XC, 2 * FFN_I], F32, s)[:, :, :],
                               spare[0][:, 0:XC * 2 * FFN_I].rearrange("p (c n) -> p c n", c=XC)]
                m["raw_d"] = [sb("raw_d", [P, FFN_I // P, D], F32, s)[:, :, :],
                              spare[1][:, 0:FFN_I // P * D].rearrange("p (c n) -> p c n", n=D)]
                m["gu"] = [sb(f"gu_{k}", [P, 2, XC, 2 * FFN_I], BF16, s) for k in hl]
                m["d"] = [sb(f"d_{k}", [P, 2, FFN_I // P, D], BF16, s) for k in hl]
                m["sg"] = sb("sg", [P, 4, TOK // E], F32, s)
                m["pr"] = sb("pr", [P, 4, TOK // E], F32, s)
                m["in"] = [oT[k][:, 0:2, :].rearrange("p s (i n) -> p s i n", n=TOK // E) for k in range(2)]
            if names[li] == "ffn1":
                m["gurow"] = sb("gurow", [P, 4, D], F32, s)
                m["M"] = sb("M", [P, 2, FI], F32, s)
                m["Q"] = sb("Q", [P, 2, FI], BF16, s)
                m["xrow"] = sb("xrow", [P, 2, D], F32, s)
                m["xM"] = sb("xM", [P, 2, D], F32, s)
                m["xQ"] = sb("xQ", [P, 2, D], BF16, s)
                m["SG"] = sb("SG", [P, 2, FI], F32, s)
                m["sB"] = sb("sB", [P, 2 * FI + D], F32, s)
                m["qxT"] = sb("qxT", [P, 2, XC, P], BF16, s)
                m["qtT"] = sb("qtT", [P, 2, IT, P], BF16, s)
                m["yt"] = sb("yt", [P, D], F32, s)
                m["row"] = sb("row", [P, 2, FI], F32, s)
                flat0 = oT[0][:, :, :].rearrange("p h n -> p (h n)")
                flat1 = oT[1][:, :, :].rearrange("p h n -> p (h n)")
                m["wT"] = flat0[:, 0:2 * XC * FI].rearrange("p (c i) -> p c i", i=FI)
                m["wdT"] = flat1[:, 0:IT * D].rearrange("p (c i) -> p c i", i=D)
            if L is None:
                s.close()
                mem.append(m)
                continue
            m["q"] = [sb(f"q{li}_{k}", [P, 2, S], BF16, s) for k in hl]
            m["k"] = [sb(f"k{li}_{k}", [P, 2, L.kv], BF16, s) for k in hl]
            m["v"] = [sb(f"v{li}_{k}", [P, 2, L.kt, HD], BF16, s) for k in hl]
            m["p"] = sb(f"p{li}", [P, 2, L.kv], F32, s)
            m["pT"] = [sb(f"pT{li}_{k}", [P, 2, 8, S], BF16, s) for k in hl]
            if L.rope:
                m["cos"], m["sin"] = sb("cos", [P, S], F32, s), sb("sin", [P, S], F32, s)
                m["rot"], m["swap"] = sb("rot", [P, 2, S], F32, s), sb("swap", [P, 2, S], F32, s)
            if L.rms:
                m["sq"] = sb("sq", [P, S], F32, s)
                m["rk"] = sb("rk", [P, 2, SC], F32, s)
                m["nq"] = sb("nq", [P, 2, QT], F32, s)
                m["g"] = sb("g", [P, 2], F32, s)
                m["mx"] = sb("mx", [P, 2], F32, s)
                m["gg"] = sb("gg", [P, 1], F32, s)
            if L.masked:
                m["m8"] = sb("m8", [P, B, SC], U8, s)
                m["mb"] = sb("mb", [P, B, SC], BF16, s)
                m["any"] = sb("any", [P, B], F32, s)
            s.close()
            mem.append(m)

        def tiles(name):
            if name == "ffn0":
                return [(4 * b + e, 4 + 2 * (e % 2) + b) for e in range(E) for b in range(B)]
            if name == "ffn1":
                return [(t, 7) for t in range(NT)]
            return [(t, t) for t in range(NT)]

        QJ = [("g", t) for t in range(IT)] + [("u", t) for t in range(IT)] + [("x", 0), ("x", 1)] + [("d", t) for t in range(D // P)]
        for t in range(NT):
            QJ += ([("x", t + 2)] if t + 2 < NT else []) + [("t", t)]
        QN = {j: k for k, j in enumerate(QJ)}
        weights_before = lambda k: sum(j[0] in "gud" for j in QJ[:k])
        gates_beside = lambda kind, t: [t - 2] if kind == "d" and t >= 2 else [t - 1] if kind == "x" and t > 2 else [t + 1] if kind == "t" and t == NT - 2 else []
        scaled_beside = lambda kind, t: [t - 2] if kind == "x" and t >= 2 else [t] if kind == "t" and t >= NT - 2 else []
        width = lambda kind: FI if kind in ("d", "t") else D
        AHEAD = 12
        GU = 2 * IT

        def quant_buffers(k):
            m, kind = mem[names.index("ffn1")], QJ[k][0]
            w = width(kind)
            if k < GU:
                flat = [t[:, :, :].rearrange("p c n -> p (c n)") for t in (xT[0], xT[1], cT[0])]
                slot = slice(k % 4 * D, k % 4 * D + D)
                return m["gurow"][:, k % 4, :], m["M"][:, :, :].rearrange("p s n -> p (s n)")[:, slot], flat[k // 8][:, k % 8 * D:k % 8 * D + D], max(0, k - 3)
            if kind == "x":
                t = QJ[k][1]
                return m["xrow"][:, t % 2, :], m["xM"][:, t % 2, :], m["xQ"][:, t % 2, :], QN[("x", t - 2)] + 1 if t >= 2 else 0
            wide = [j for j in range(GU, k + 1) if QJ[j][0] in "dt"]
            i = (len(wide) - 1) % 2
            return m["row"][:, i, :], m["M"][:, i, :], m["Q"][:, i, :], wide[-3] + 1 if len(wide) > 2 else GU

        def diag(k):
            flat = [cT[1][:, :, :].rearrange("p c n -> p (c n)")] + [t[:, :, :].rearrange("p c n -> p (c n)") for t in wkv]
            t, o = (flat[0], k) if k < 16 else (flat[1 + (k - 16) // 8], (k - 16) % 8)
            return t.bitcast(F32)[:, o * P:o * P + P]

        CH = [(0, 512), (512, 1024), (1024, FI)]

        block = ctx.enter_context(nc.Block())

        @block.sync
        def _(sp):
            sp.dma_start(xf[:, :, :], a["x"].rearrange("b (p e) d -> p b e d", e=4)).then_inc(x_in, 16)
            sp.dma_start(idx[:, :], a["didx"]).then_inc(idx_in, 16)
            for li, L in enumerate(stages):
                if names[li] == "ffn0":
                    m = mem[li]
                    sp.wait_ge(job_mm, ledger[li]["job"])
                    for e in range(E):
                        if e == 1:
                            sp.wait_ge(y_mm, ledger[li]["ln"])
                        if e >= 2:
                            sp.wait_ge(gate_lo, e - 1)
                            sp.wait_ge(up_lo, e - 1)
                        sp.dma_start(m["raw_gu"][e % 2], a["gu"][e]).then_inc(gu_in[e % 2], 16)
                        if e >= 2:
                            sp.wait_ge(d_lo, e - 1)
                        sp.dma_start(m["raw_d"][e % 2], a["down"][e]).then_inc(d_in[e % 2], 16)
                    continue
                if names[li] == "ffn1":
                    m = mem[li]
                    for t in range(D // P):
                        k = QN[("d", t)]
                        if t >= 2:
                            sp.wait_ge(q_ok, quant_buffers(k)[3])
                        sp.dma_start(quant_buffers(k)[0], a["wdown"][t * P:(t + 1) * P, :]).then_inc(rowd_in, 16)
                        sp.wait_ge(rowd_in, 16 * (t + 1))
                    continue
                c, base = ledger[li], ledger[li]["split"]
                if L.rope:
                    sp.dma_start(mem[li]["cos"][:, :], a["cos"]).then_inc(const_in, 16)
                    sp.dma_start(mem[li]["sin"][:, :], a["sin"]).then_inc(const_in, 16)
                if L.name == "cross0":
                    for k in range(4):
                        sp.wait_ge(w_split, base - 4 + k - 1)
                        sp.dma_start(raw_kv[:, k % 2, :], a["ctxT"][:, k, :]).then_inc(w_in[k % 2], 16)
                cols = 2 * L.chunks * HD

                def qkv(g, j, free):
                    if free is not None:
                        sp.wait_ge(w_split, free)
                    sp.dma_start(raw_q[:, j, :], a["wq" + L.name][bass.ds(2 * g + j, 1), :, :].rearrange("o p n -> p (o n)")).then_inc(w_in[j], 16)
                    if not L.gqa:
                        sp.dma_start(raw_kv[:, j, 0:cols], a["wkv" + L.name][bass.ds(2 * g + j, 1), :, :].rearrange("o p n -> p (o n)")).then_inc(w_in[j], 16)
                    elif j == 0:
                        sp.dma_start(raw_kv[:, j, 0:cols], a["wkv" + L.name][bass.ds(g, 1), :, :].rearrange("o p n -> p (o n)")).then_inc(w_in[j], 16)

                for j in range(2):
                    qkv(0, j, None if li == 0 else base + j - 1)
                if L.rms:
                    sp.wait_ge(ln_x, NT * li)
                    sp.dma_start(mem[li]["g"][:, :], a["gqk"]).then_inc(const_in, 16)
                if L.masked:
                    sp.wait_ge(ln_x, NT * li)
                    sp.dma_start(mem[li]["m8"][:, :, :], a["mask"].partition_broadcast(P)).then_inc(const_in, 16)
                with sp.Fori(1, H // 2) as g:
                    for j in range(2):
                        qkv(g, j, g * 2 + (base + j - 1))
                with sp.Fori(0, H // 2) as g:
                    for j in range(2):
                        sp.wait_ge(w_split, g * 2 + (base + H + j - 1))
                        sp.dma_start(raw_q[:, j, :], a["wo" + L.name][bass.ds(2 * g + j, 1), :, :].rearrange("o p n -> p (o n)")).then_inc(w_in[j], 16)
            sp.wait_ge(ln_x, NT * len(stages))
            sp.dma_start(out.rearrange("b (p e) d -> p b e d", e=4), xf[:, :, :]).then_inc(out_ok, 16)
            sp.wait_ge(out_ok, 16)

        @block.gpsimd
        def _(pool):
            nseq = [0]

            def own(ins):
                nseq[0] += 1
                ins.then_inc(pool_seq, 1)
                pool.wait_ge(pool_seq, nseq[0])

            own(nc.gpsimd.memset(ident[:, :], 0.0))
            nc.gpsimd.affine_select(out=ident[:, :], in_=ident[:, :], compare_op=ALU.not_equal, fill=1.0,
                                    base=0, pattern=[[-1, P]], channel_multiplier=1).then_inc(const_ok, 1)
            own(nc.gpsimd.memset(causal_bias[:, :], 0.0))
            nc.gpsimd.affine_select(out=causal_bias[:, :], in_=causal_bias[:, :], compare_op=ALU.is_ge, fill=NEG,
                                    base=384, pattern=[[-1, 512]], channel_multiplier=1).then_inc(const_ok, 1)
            nc.gpsimd.memset(half_neg[:, :], -0.5).then_inc(const_ok, 1)
            nc.gpsimd.memset(ones[:, :], 1.0).then_inc(const_ok, 1)
            pool.wait_ge(const_ok, 4)
            nc.gpsimd.tensor_scalar(idb[:, :], ident[:, :], 1.0, 1.0, ALU.mult, ALU.mult).then_inc(idb_ok, 1)

            def split_item(pairs, waits, item):
                for s, v in waits:
                    pool.wait_ge(s, v)
                pool.nop(nofuse=True)
                for dst, src in pairs:
                    last = nc.gpsimd.tensor_scalar(dst[0], src, 1.0, 1.0, ALU.mult, ALU.mult)
                last.then_inc(w_hi, 1)
                pool.wait_ge(w_hi, item)
                for dst, src in pairs:
                    last = nc.gpsimd.tensor_tensor(dst[1], src, dst[0], ALU.subtract)
                last.then_inc(w_split, 1)

            def qkv_splitter(li):
                L = stages[li]
                cols = 2 * L.chunks * HD

                def split_qkv(j, value, used, item):
                    pairs = [((wq[0][:, j, :, :].rearrange("p c d -> p (c d)"), wq[1][:, j, :, :].rearrange("p c d -> p (c d)")), raw_q[:, j, :])]
                    if not L.gqa or j == 0:
                        pairs.append(((wkv[0][:, j, 0:cols], wkv[1][:, j, 0:cols]), raw_kv[:, j, 0:cols]))
                    split_item(pairs, [(w_in[j], value)] + ([(job_mm, used)] if used is not None else []), item)
                return split_qkv

            def start_layer(li):
                L, c, m = stages[li], ledger[li], mem[li]
                if L.name == "cross0":
                    for k in range(4):
                        half, chunk = k // 2, k % 2
                        sl = slice(half * SC, (half + 1) * SC)
                        split_item([((cT[0][:, chunk, sl], cT[1][:, chunk, sl]), raw_kv[:, k % 2, :])],
                                   [(w_in[k % 2], c[f"win{k % 2}"] - 32 + 16 * (k // 2 + 1))], c["split"] - 4 + k + 1)
                split_qkv = qkv_splitter(li)
                for j in range(2):
                    split_qkv(j, c[f"win{j}"] + (32 if j == 0 or not L.gqa else 16), c["job"] if li else None, c["split"] + j + 1)

            def gather(k):
                kind, t = QJ[k]
                nc.gpsimd.indirect_dma_start(out=quant_buffers(k)[0], out_offset=None, in_=a["wgate" if kind == "g" else "wup"],
                                             in_offset=bass.IndirectOffsetOnAxis(ap=idx[:, t:t + 1].bitcast(mybir.dt.uint32), axis=0)).then_inc(row_in[k % 4], 16)

            def round_rows(k):
                y, M, q, _ = quant_buffers(k)
                pool.wait_ge(q_m, k + 1)
                nc.gpsimd.tensor_tensor(q, y, M, ALU.subtract).then_inc(q_ok, 1)
                if k + 4 < GU:
                    pool.wait_ge(q_ok, k + 1)
                    gather(k + 4)

            for li, L in enumerate(stages):
                c, m = ledger[li], mem[li]

                def inv_std(k):
                    t = tiles(names[li])[k][0]
                    pool.wait_ge(ln_var, c["ln"] + k + 1)
                    own(nc.gpsimd.tensor_scalar(rstd[:, t:t + 1], mv[:, t, 1:2], EPS, None, ALU.add))
                    nc.gpsimd.tensor_tensor(rstd[:, t:t + 1], rstd[:, t:t + 1], half_neg[:, 0:1], ALU.pow).then_inc(ln_rstd, 1)

                if L is not None and L.rms:
                    pool.wait_ge(const_in, 48)
                    nc.gpsimd.tensor_tensor(m["gg"][:, :], m["g"][:, 0:1], m["g"][:, 1:2], ALU.mult).then_inc(const_ok, 1)
                if L is not None and L.masked:
                    pool.wait_ge(const_in, 64)
                    nc.gpsimd.tensor_scalar(m["mb"][:, :, :], m["m8"][:, :, :], -NEG, NEG, ALU.mult, ALU.add).then_inc(const_ok, 1)

                if names[li] == "ffn0":
                    def gate_low(e):
                        pool.wait_ge(gu_hi, e + 1)
                        nc.gpsimd.tensor_tensor(m["gu"][1][:, e % 2, :, 0:FFN_I], m["raw_gu"][e % 2][:, :, 0:FFN_I], m["gu"][0][:, e % 2, :, 0:FFN_I], ALU.subtract).then_inc(gate_lo, 1)
                    gate_low(0)
                    for e in range(E + 1):
                        if e + 1 < E:
                            gate_low(e + 1)
                        if e == E:
                            start_layer(li + 1)
                        if e:
                            inv_std(2 * e - 2)
                            inv_std(2 * e - 1)
                    continue
                if names[li] == "ffn1":
                    for k in range(GU, len(QJ)):
                        kind, t = QJ[k]
                        for u in gates_beside(kind, t):
                            pool.wait_ge(fs_ok, u + 1)
                            nc.gpsimd.tensor_tensor(m["SG"][:, u % 2, :], m["SG"][:, u % 2, :], m["sB"][:, FI:2 * FI], ALU.mult).then_inc(gs_ok, 1)
                        y, M, q, before = quant_buffers(k)
                        pool.wait_ge(q_m, k + 1)
                        nc.gpsimd.tensor_tensor(y, y, M, ALU.add).then_inc(q_w, 1)
                        if before > GU:
                            pool.wait_ge(q_mm, before)
                        pool.wait_ge(q_w, k - GU + 1)
                        nc.gpsimd.tensor_tensor(q, y, M, ALU.subtract).then_inc(q_ok, 1)
                        if kind == "t" and t:
                            inv_std(t - 1)
                    inv_std(NT - 1)
                    continue
                cols = 2 * L.chunks * HD
                pT = m["pT"]

                if not li:
                    start_layer(li)
                split_qkv = qkv_splitter(li)
                def query_norms(n, it, qt, jobs):
                    for x, (kind, _) in enumerate(jobs):
                        if kind == "QN":
                            pool.wait_ge(job_lo, at(lambda n: c["lo"] + L.before(n, qt) + x + 1, n, it))
                            r = m["nq"][:, (n + 1) % 2, :]
                            nc.gpsimd.tensor_tensor(r, r, half_neg[:, 0:QT], ALU.pow).then_inc(q_norm, 1)

                def rope(n, it, qt, jobs):
                    for x, (kind, _) in enumerate(jobs):
                        if kind not in ("K", "Q"):
                            continue
                        r = ("Q", "K").index(kind)
                        hi = lambda n: c["hi"] + L.before(n, qt, BY_ACT) + x + 1
                        lo = lambda n: c["lo"] + L.before(n, qt) + x + 1
                        pool.wait_ge(job_hi, at(hi, n, it))
                        nc.gpsimd.tensor_tensor(m["swap"][:, r, :], m["swap"][:, r, :], m["sin"][:, :], ALU.mult).then_inc(rope_mul, 1)
                        pool.wait_ge(rope_mul, at(lambda n: c["rope"] + 2 * (n + 1) + r + 1, n, it))
                        pool.wait_ge(job_lo, at(lo, n, it))
                        nc.gpsimd.tensor_tensor(m["rot"][:, r, :], m["rot"][:, r, :], m["swap"][:, r, :], ALU.add).then_inc(rope_sum, 1)

                def unit(n, it):
                    if n % 4 >= 2 and n // 4 < H // 2 - 1:
                        j = n % 4 - 2
                        value = lambda n: c[f"win{j}"] + (32 if j == 0 or not L.gqa else 16) * (n // 4 + 2)
                        split_qkv(j, at(value, n, it), at(lambda n: c["job"] + L.before(n), n, it),
                                  at(lambda n: c["split"] + 2 * (n // 4) + 2 + j + 1, n, it))
                    for qt in range(QT):
                        w = P * (qt + 1) if L.causal else L.kv
                        s = lambda n: c["s"] + QT * n + qt + 1
                        pool.wait_ge(r_inv, at(s, n, it))
                        pool.nop(nofuse=True)
                        nc.gpsimd.tensor_scalar(m["p"][:, qt % 2, 0:w], m["p"][:, qt % 2, 0:w], ri[:, qt % 2:qt % 2 + 1], 1.0,
                                                ALU.mult, ALU.mult).then_inc(p_norm, 1)
                        if L.rope:
                            rope(n, it, qt, L.jobs(n, qt))
                        if L.rms:
                            query_norms(n, it, qt, L.jobs(n, qt))

                for qt in range(QT):
                    if L.rope:
                        rope(-1, None, qt, L.jobs(-1, qt))
                    if L.rms:
                        query_norms(-1, None, qt, L.jobs(-1, qt))
                units(pool, unit)

                last_attention = names[li + 1:li + 2] == ["ffn1"]
                for slot in range(2):
                    n_pv = c["job"] + (L.before(UNITS) if slot == 0 else L.before(UNITS + 1))
                    pool.wait_ge(job_mm, n_pv)
                    if last_attention and slot == 1:
                        pool.wait_ge(idx_in, 16)
                        for k in range(4):
                            gather(k)
                    for k in range(8):
                        h, j = 8 * slot + k, k % 2
                        win = c[f"win{j}"] + 16 * (H // 2) * (1 if L.gqa and j == 1 else 2) + 16 * (h // 2 + 1)
                        split_item([((pT[0][:, slot, k, :], pT[1][:, slot, k, :]), raw_q[:, j, :])], [(w_in[j], win)], c["split"] + H + h + 1)
                        if last_attention and slot == 1:
                            round_rows(k)

                if li + 1 < len(stages) and stages[li + 1] is not None:
                    start_layer(li + 1)
                done = 8
                for t in range(NT):
                    if last_attention:
                        for k in range(done, AHEAD + t):
                            round_rows(k)
                        done = AHEAD + t
                    inv_std(t)
                if last_attention:
                    for k in range(done, GU):
                        round_rows(k)

        @block.scalar
        def _(act):
            def x_part(n, t, bank):
                act.wait_ge(x_mm, n + 1)
                b, e = t // 4, t % 4
                nc.scalar.activation(xT[0][:, :, b * S + e:(b + 1) * S:4], ps[:, bank, :].rearrange("p (c n) -> p c n", c=XC), ACT.Copy).then_inc(x_hi, 1)

            nc.scalar.preload_act_table_set("natural_log_exp_and_others")
            for t in range(NT):
                x_part(t, t, t)
            for li, L in enumerate(stages):
                c, m = ledger[li], mem[li]
                if L is not None and li:
                    nc.scalar.preload_act_table_set("natural_log_exp_and_others")
                if names[li] == "ffn0":
                    def gu_high(e):
                        if e >= 2:
                            act.wait_ge(gu_mm, 4 * (e - 1))
                        act.wait_ge(gu_in[e % 2], 16 * (e // 2 + 1))
                        nc.scalar.activation(m["gu"][0][:, e % 2, :, :], m["raw_gu"][e % 2], ACT.Copy).then_inc(gu_hi, 1)

                    def down_high(e):
                        if e >= 2:
                            act.wait_ge(y_mm, c["ln"] + 2 * (e - 1))
                        act.wait_ge(d_in[e % 2], 16 * (e // 2 + 1))
                        nc.scalar.activation(m["d"][0][:, e % 2, :, :], m["raw_d"][e % 2], ACT.Copy).then_inc(d_hi, 1)

                    gu_high(0)
                    down_high(0)
                    for e in range(E + 2):
                        if e < E:
                            for i in range(4):
                                if i == 2 and e + 1 < E:
                                    gu_high(e + 1)
                                act.wait_ge(gu_mm, 4 * e + i + 1)
                                if e:
                                    act.wait_ge(prod_ok, 4 * (e - 1) + i + 1)
                                nc.scalar.activation(m["sg"][:, i, :], ps[:, i, 0:TOK // E], ACT.Silu).then_inc(silu_ok, 1)
                            act.wait_ge(prod_ok, 4 * (e + 1))
                            nc.scalar.activation(m["in"][0][:, e % 2, :, :], m["pr"][:, :, :], ACT.Copy).then_inc(inter_hi, 1)
                        if e >= 2:
                            for k in (2 * e - 4, 2 * e - 3):
                                x_part(NT + c["ln"] + k, *tiles("ffn0")[k])
                        if e + 1 < E:
                            down_high(e + 1)
                    continue
                if names[li] == "ffn1":
                    for k, (kind, t) in enumerate(QJ):
                        for u in gates_beside(kind, t):
                            act.wait_ge(g_ok, u + 1)
                            sx = q_scale[:, QN[("x", u)]:QN[("x", u)] + 1]
                            nc.scalar.activation(m["SG"][:, u % 2, :], m["SG"][:, u % 2, :], ACT.Silu, scale=sx).then_inc(fs_ok, 1)
                        for u in scaled_beside(kind, t):
                            y, n = quant_buffers(QN[("t", u)])[0], QN[("t", u)]
                            act.wait_ge(q_a, GU + u + 1)
                            nc.scalar.activation(y, y, ACT.Copy, scale=q_inv[:, n:n + 1]).then_inc(q_s, 1)
                        act.wait_ge(q_mm, k + 1)
                        lo = ps[:, 6 + (k % 2 if k < GU else 0), :].bitcast(BF16).rearrange("p (c n) -> p c n", n=P)
                        hi = ps[:, 7, :].bitcast(BF16).rearrange("p (c n) -> p c n", n=P)
                        if kind in "gu":
                            o = XC if kind == "u" else 0
                            nc.scalar.activation(m["wT"][:, o:o + XC, t * P:(t + 1) * P], lo[:, 0:XC, :], ACT.Copy).then_inc(q_T, 1)
                        elif kind == "x":
                            nc.scalar.activation(m["qxT"][:, t % 2, :, :], lo[:, 0:XC, :], ACT.Copy).then_inc(q_T, 1)
                        else:
                            dst = m["wdT"][:, :, t * P:(t + 1) * P] if kind == "d" else m["qtT"][:, t % 2, :, :]
                            nc.scalar.activation(dst[:, 0:8, :], lo[:, :, :], ACT.Copy)
                            if kind == "d":
                                act.wait_ge(diag_mm, GU + t + 1)
                            nc.scalar.activation(dst[:, 8:IT, :], hi[:, 0:IT - 8, :], ACT.Copy).then_inc(q_T, 1)
                        if kind in "gud":
                            act.wait_ge(diag_mm, weights_before(k) + 1)
                            bank = ps[:, 7, 3 * P:4 * P] if kind == "d" else ps[:, 4 + k % 2, 0:P]
                            o = {"g": 0, "u": FI, "d": 2 * FI}[kind] + t * P
                            nc.scalar.activation(m["sB"][:, o:o + P], bank, ACT.Copy).then_inc(diag_cp, 1)
                    continue

                def job_parts(n, it, qt, jobs):
                    b, u = L.batch(n + 1), n + 1
                    for x, (kind, half) in enumerate(jobs):
                        if kind not in BY_ACT:
                            continue
                        bank = ps[:, M_BANK + (L.before(n, qt) + x) % 2, :]
                        act.wait_ge(job_mm, at(lambda n: c["job"] + L.before(n, qt) + x + 1, n, it))
                        if kind == "PV":
                            h = at(L.head, n - 1, it)
                            pb = L.batch(n - 1)
                            o = oT[0][:, bass.ds(h, 1), pb * S:(pb + 1) * S]
                            src = bank.rearrange("p (o n) -> p o n", o=1)
                            if L.masked:
                                nc.scalar.activation(o, src, ACT.Copy, scale=m["any"][:, pb:pb + 1]).then_inc(job_hi, 1)
                            else:
                                nc.scalar.activation(o, src, ACT.Copy).then_inc(job_hi, 1)
                        elif kind == "V":
                            nc.scalar.activation(m["v"][0][:, L.kvslot(u), 4 * half:4 * half + 4, :], bank.rearrange("p (t d) -> p t d", d=HD), ACT.Copy).then_inc(job_hi, 1)
                        elif L.rope:
                            r = ("Q", "K").index(kind)
                            nc.scalar.activation(m["swap"][0:64, r, :], bank[64:128, :], ACT.Copy)
                            nc.scalar.activation(m["swap"][64:128, r, :], bank[0:64, :], ACT.Copy).then_inc(job_hi, 1)
                        else:
                            if L.rms:
                                nc.scalar.activation(m["sq"][:, :], bank, ACT.Square).then_inc(sq_ok, 1)
                            if kind == "Q":
                                nc.scalar.activation(m["q"][0][:, u % 2, :], bank, ACT.Copy).then_inc(job_hi, 1)
                            else:
                                o = m["k"][0][:, L.kvslot(u), half * 512:half * 512 + 512]
                                if L.rms:
                                    nc.scalar.activation(o, bank, ACT.Copy, scale=m["gg"][:, 0:1]).then_inc(job_hi, 1)
                                else:
                                    nc.scalar.activation(o, bank, ACT.Copy).then_inc(job_hi, 1)

                def key_norms(n, it, qt, jobs):
                    for x, (kind, half) in enumerate(jobs):
                        if (kind, half) == ("KN", 1):
                            act.wait_ge(job_lo, at(lambda n: c["lo"] + L.before(n, qt) + x + 1, n, it))
                            r = m["rk"][:, (n + 1) % 2, :]
                            nc.scalar.activation(r, r, ACT.Ln).then_inc(k_log, 1)
                            act.wait_ge(k_log, at(lambda n: n + 2, n, it))
                            nc.scalar.activation(r, r, ACT.Exp, scale=-0.5).then_inc(k_norm, 1)

                def rotated(n, it, qt, jobs):
                    for kind, _ in jobs:
                        if kind in ("K", "Q"):
                            r = ("Q", "K").index(kind)
                            act.wait_ge(rope_sum, at(lambda n: c["rope"] + 2 * (n + 1) + r + 1, n, it))
                            nc.scalar.activation(m[kind.lower()][0][:, (n + 1) % 2, :], m["rot"][:, r, :], ACT.Copy).then_inc(rope_hi, 1)

                def turned(n, it, qt):
                    for half in range(L.halves):
                        blocks = qt + 1 if L.causal else 4
                        idx = lambda n: c["x"] + (QT * n + qt) * L.halves + half
                        act.wait_ge(t_mm, at(lambda n: idx(n) + 1, n, it))
                        bank = ps[:, T_BANK + idx(n) % 2, 0:blocks * P].rearrange("p (k q) -> p k q", q=P)
                        nc.scalar.activation(m["pT"][0][:, n % 2, 4 * half:4 * half + blocks, qt * P:qt * P + P], bank, ACT.Copy).then_inc(t_hi, 1)

                def unit(n, it):
                    for qt in range(QT):
                        w = P * (qt + 1) if L.causal else L.kv
                        act.wait_ge(s_max, at(lambda n: CREDIT + c["s"] + QT * n + qt + 1, n, it))
                        prob = m["p"][:, qt % 2, 0:w]
                        nc.scalar.activation(prob, prob, ACT.Exp, scale=1.0 if L.rms else -1.0, bias=nb[:, qt % 2:qt % 2 + 1], accum_out=rs[:, qt % 2:qt % 2 + 1]).then_inc(p_exp, 1)
                        job_parts(n, it, qt, L.jobs(n, qt))
                        if L.rope and qt > 0:
                            rotated(n, it, qt - 1, L.jobs(n, qt - 1))
                        if qt > 0:
                            turned(n, it, qt - 1)
                        elif n > 0:
                            turned(n - 1, it, QT - 1)
                        if L.rms:
                            key_norms(n, it, qt, L.jobs(n, qt))

                if L.rms:
                    act.wait_ge(const_ok, 5)
                if L.masked:
                    act.wait_ge(const_ok, 7)
                for qt in range(QT):
                    job_parts(-1, None, qt, L.jobs(-1, qt))
                    if L.rope:
                        rotated(-1, None, qt, L.jobs(-1, qt))
                    if L.rms:
                        key_norms(-1, None, qt, L.jobs(-1, qt))
                units(act, unit)
                turned(UNITS - 1, None, QT - 1)
                for qt in range(QT):
                    job_parts(UNITS, None, qt, L.jobs(UNITS, qt))
                if names[li + 1:li + 2] != ["ffn1"]:
                    for t in range(NT):
                        x_part(NT * (li + 1) + t, t, t)
                else:
                    for k in range(GU):
                        y = quant_buffers(k)[0]
                        act.wait_ge(q_a, k + 1)
                        nc.scalar.activation(diag(k), ident[:, :], ACT.Copy, scale=q_scale[:, k:k + 1]).then_inc(diag_ok, 1)
                        nc.scalar.activation(y, y, ACT.Copy, scale=q_inv[:, k:k + 1]).then_inc(q_s, 1)

        @block.vector
        def _(dve):
            nseq = [0]

            def own(ins):
                nseq[0] += 1
                ins.then_inc(dve_seq, 1)
                dve.wait_ge(dve_seq, nseq[0])

            dve.sem_inc(job_lo, CREDIT)
            dve.sem_inc(s_max, CREDIT)
            dve.sem_inc(t_lo, CREDIT)

            def x_part(n, t, bank):
                dve.wait_ge(x_hi, n + 1)
                b, e = t // 4, t % 4
                sl = slice(b * S + e, (b + 1) * S, 4)
                nc.vector.tensor_tensor(xT[1][:, :, sl], ps[:, bank, :].rearrange("p (c n) -> p c n", c=XC), xT[0][:, :, sl], ALU.subtract).then_inc(x_lo, 1)

            for t in range(NT):
                x_part(t, t, t)

            def round_gu(k):
                if k + 1 < GU:
                    quantise(k + 1)
                y, M, _, _ = quant_buffers(k)
                dve.wait_ge(q_s, k + 1)
                own(nc.vector.tensor_scalar(M.bitcast(I32), y.bitcast(I32), 0x7F800000, None, ALU.bitwise_and))
                own(nc.vector.tensor_scalar(M, M, 2.0 ** -6, 1.5 * 2.0 ** 20, ALU.max, ALU.mult))
                nc.vector.tensor_tensor(y, y, M, ALU.add).then_inc(q_m, 1)

            def quantise(k):
                (kind, t), m = QJ[k], mem[names.index("ffn1")]
                (y, M, _, free), col = quant_buffers(k), slice(k, k + 1)
                if free > 0:
                    dve.wait_ge(q_ok, free)
                for u in [t - 2] if kind == "d" and t >= 2 else [t + 1] if kind == "t" and 0 < t < NT - 1 else []:
                    dve.wait_ge(diag_cp, GU)
                    dve.wait_ge(fg_mm, u + 1)
                    if u >= 2:
                        dve.wait_ge(row_y, u - 1)
                    nc.vector.tensor_tensor(m["SG"][:, u % 2, :], ps[:, 0:3, :].rearrange("p a n -> p (a n)")[:, 0:FI], m["sB"][:, 0:FI], ALU.mult).then_inc(g_ok, 1)
                if kind in "gu":
                    dve.wait_ge(row_in[k % 4], 16 * (k // 4 + 1))
                elif kind == "d":
                    dve.wait_ge(rowd_in, 16 * (t + 1))
                elif kind == "t":
                    dve.wait_ge(fu_mm, t + 1)
                    dve.wait_ge(gs_ok, t + 1)
                    sx = q_scale[:, QN[("x", t)]:QN[("x", t)] + 1]
                    nc.vector.scalar_tensor_tensor(out=y, in0=ps[:, 3:6, :].rearrange("p a n -> p (a n)")[:, 0:FI], scalar=sx, in1=m["SG"][:, t % 2, :], op0=ALU.mult, op1=ALU.mult).then_inc(row_y, 1)
                    dve.wait_ge(row_y, t + 1)
                if kind in "gut":
                    own(nc.vector.tensor_reduce(q_max[:, col], y, AX.X, ALU.max, apply_absolute_value=True))
                    own(nc.vector.tensor_scalar(q_scale[:, col], q_max[:, col], 1.0 / FP8_MAX, None, ALU.mult))
                    nc.vector.reciprocal(q_inv[:, col], q_scale[:, col]).then_inc(q_a, 1)
                    return
                src = xf[:, t, :] if kind == "x" else y
                own(nc.vector.tensor_reduce(q_max[:, col], src, AX.X, ALU.max, apply_absolute_value=True))
                nc.vector.tensor_scalar(q_scale[:, col], q_max[:, col], 1.0 / FP8_MAX, None, ALU.mult)
                own(nc.vector.reciprocal(q_inv[:, col], q_max[:, col]))
                own(nc.vector.tensor_scalar(y, src, q_inv[:, col], FP8_MAX, ALU.mult, ALU.mult))
                own(nc.vector.tensor_scalar(M.bitcast(I32), y.bitcast(I32), 0x7F800000, None, ALU.bitwise_and))
                nc.vector.tensor_scalar(M, M, 2.0 ** -6, 1.5 * 2.0 ** 20, ALU.max, ALU.mult).then_inc(q_m, 1)
                if kind == "d":
                    nc.vector.tensor_scalar(diag(k), ident[:, :], q_scale[:, col], None, ALU.mult).then_inc(diag_ok, 1)

            for li, L in enumerate(stages):
                c, m = ledger[li], mem[li]

                def residual(k):
                    t, bank = tiles(names[li])[k]
                    dve.wait_ge(y_mm, c["ln"] + k + 1)
                    if names[li] == "ffn1":
                        dve.wait_ge(diag_cp, weights_before(len(QJ)))
                        n = QN[("t", t)]
                        ins = nc.vector.scalar_tensor_tensor(out=m["yt"][:, :], in0=ps[:, bank, :], scalar=q_scale[:, n:n + 1], in1=m["sB"][:, 2 * FI:2 * FI + D],
                                                             op0=ALU.mult, op1=ALU.mult)
                        ins.then_inc(fy_ok, 1)
                        dve.wait_ge(fy_ok, k + 1)
                        own(nc.vector.tensor_tensor(xf[:, t, :], m["yt"][:, :], xf[:, t, :], ALU.add))
                    else:
                        own(nc.vector.tensor_tensor(xf[:, t, :], ps[:, bank, :], xf[:, t, :], ALU.add))
                    own(nc.vector.bn_stats(stat[:, t, :], xf[:, t, :]))
                    nc.vector.bn_aggr(mv[:, t, :], stat[:, t, :]).then_inc(ln_var, 1)

                def normalise(k):
                    t = tiles(names[li])[k][0]
                    dve.wait_ge(ln_rstd, c["ln"] + k + 1)
                    dve.wait_ge(ln_var, c["ln"] + k + 1)
                    nc.vector.tensor_scalar(xf[:, t, :], xf[:, t, :], mv[:, t, 0:1], rstd[:, t:t + 1], ALU.subtract, ALU.mult).then_inc(ln_x, 1)

                if names[li] == "ffn0":
                    def up_low(e):
                        dve.wait_ge(gu_hi, e + 1)
                        nc.vector.tensor_tensor(m["gu"][1][:, e % 2, :, FFN_I:2 * FFN_I], m["raw_gu"][e % 2][:, :, FFN_I:2 * FFN_I], m["gu"][0][:, e % 2, :, FFN_I:2 * FFN_I],
                                                ALU.subtract).then_inc(up_lo, 1)

                    def down_low(e):
                        dve.wait_ge(d_hi, e + 1)
                        nc.vector.tensor_tensor(m["d"][1][:, e % 2, :, :], m["raw_d"][e % 2], m["d"][0][:, e % 2, :, :], ALU.subtract).then_inc(d_lo, 1)

                    up_low(0)
                    down_low(0)
                    for e in range(E + 2):
                        if e < E:
                            for i in range(4):
                                if i == 2 and e + 1 < E:
                                    up_low(e + 1)
                                dve.wait_ge(silu_ok, 4 * e + i + 1)
                                if e:
                                    dve.wait_ge(inter_hi, e)
                                    dve.wait_ge(inter_lo, e)
                                nc.vector.tensor_tensor(m["pr"][:, i, :], ps[:, i, TOK // E:2 * TOK // E], m["sg"][:, i, :], ALU.mult).then_inc(prod_ok, 1)
                            dve.wait_ge(inter_hi, e + 1)
                            nc.vector.tensor_tensor(m["in"][1][:, e % 2, :, :], m["pr"][:, :, :], m["in"][0][:, e % 2, :, :], ALU.subtract).then_inc(inter_lo, 1)
                        if e >= 2:
                            for k in (2 * e - 4, 2 * e - 3):
                                x_part(NT + c["ln"] + k, *tiles("ffn0")[k])
                        if 1 <= e <= E:
                            residual(2 * e - 2)
                            residual(2 * e - 1)
                            normalise(2 * e - 2)
                            normalise(2 * e - 1)
                        if e + 1 < E:
                            down_low(e + 1)
                    continue
                if names[li] == "ffn1":
                    for k in range(GU, len(QJ)):
                        kind, t = QJ[k]
                        for u in scaled_beside(kind, t):
                            quantise(QN[("t", u)])
                        if kind != "t":
                            quantise(k)
                        else:
                            y, M, _, _ = quant_buffers(k)
                            dve.wait_ge(q_s, GU + t + 1)
                            own(nc.vector.tensor_scalar(M.bitcast(I32), y.bitcast(I32), 0x7F800000, None, ALU.bitwise_and))
                            nc.vector.tensor_scalar(M, M, 2.0 ** -6, 1.5 * 2.0 ** 20, ALU.max, ALU.mult).then_inc(q_m, 1)
                        if kind == "t" and t:
                            residual(t - 1)
                        if kind == "t" and t > 1:
                            normalise(t - 2)
                    residual(NT - 1)
                    normalise(NT - 2)
                    normalise(NT - 1)
                    continue

                def job_parts(n, it, qt, jobs):
                    u = n + 1
                    for x, (kind, half) in enumerate(jobs):
                        bank = ps[:, M_BANK + (L.before(n, qt) + x) % 2, :]
                        acts = sum(k in BY_ACT for k, _ in jobs[:x + 1])
                        if kind in BY_ACT:
                            dve.wait_ge(job_hi, at(lambda n: c["hi"] + L.before(n, qt, BY_ACT) + acts, n, it))
                        else:
                            dve.wait_ge(job_mm, at(lambda n: c["job"] + L.before(n, qt) + x + 1, n, it))
                        if kind == "PV":
                            h = at(L.head, n - 1, it)
                            pb = L.batch(n - 1)
                            o, hi = (oT[k][:, bass.ds(h, 1), pb * S:(pb + 1) * S] for k in (1, 0))
                            src = bank.rearrange("p (o n) -> p o n", o=1)
                            if L.masked:
                                nc.vector.scalar_tensor_tensor(out=o, in0=src, scalar=m["any"][:, pb:pb + 1], in1=hi, op0=ALU.mult, op1=ALU.subtract).then_inc(job_lo, 1)
                            else:
                                nc.vector.tensor_tensor(o, src, hi, ALU.subtract).then_inc(job_lo, 1)
                        elif kind == "V":
                            o, hi = (m["v"][k][:, L.kvslot(u), 4 * half:4 * half + 4, :] for k in (1, 0))
                            nc.vector.tensor_tensor(o, bank.rearrange("p (t d) -> p t d", d=HD), hi, ALU.subtract).then_inc(job_lo, 1)
                        elif kind == "KN":
                            nc.vector.tensor_scalar(m["rk"][:, u % 2, half * 512:half * 512 + 512], bank, 1.0 / HD, EPS, ALU.mult, ALU.add).then_inc(job_lo, 1)
                        elif kind == "QN":
                            nc.vector.tensor_scalar(m["nq"][:, u % 2, :], bank[:, 0:QT], 1.0, EPS * HD, ALU.mult, ALU.add).then_inc(job_lo, 1)
                        elif L.rope:
                            r = ("Q", "K").index(kind)
                            nc.vector.tensor_tensor(m["rot"][:, r, :], bank, m["cos"][:, :], ALU.mult).then_inc(job_lo, 1)
                        elif kind == "Q":
                            nc.vector.tensor_tensor(m["q"][1][:, u % 2, :], bank, m["q"][0][:, u % 2, :], ALU.subtract).then_inc(job_lo, 1)
                        else:
                            o, hi = (m["k"][k][:, L.kvslot(u), half * 512:half * 512 + 512] for k in (1, 0))
                            if L.rms:
                                nc.vector.scalar_tensor_tensor(out=o, in0=bank, scalar=m["gg"][:, 0:1], in1=hi, op0=ALU.mult, op1=ALU.subtract).then_inc(job_lo, 1)
                            else:
                                nc.vector.tensor_tensor(o, bank, hi, ALU.subtract).then_inc(job_lo, 1)

                def rotated(n, it, qt, jobs):
                    for kind, _ in jobs:
                        if kind in ("K", "Q"):
                            r = ("Q", "K").index(kind)
                            dve.wait_ge(rope_hi, at(lambda n: c["rope"] + 2 * (n + 1) + r + 1, n, it))
                            o, hi = (m[kind.lower()][k][:, (n + 1) % 2, :] for k in (1, 0))
                            nc.vector.tensor_tensor(o, m["rot"][:, r, :], hi, ALU.subtract).then_inc(rope_lo, 1)

                def turned(n, it, qt):
                    for half in range(L.halves):
                        blocks = qt + 1 if L.causal else 4
                        idx = lambda n: c["x"] + (QT * n + qt) * L.halves + half
                        dve.wait_ge(t_hi, at(lambda n: idx(n) + 1, n, it))
                        bank = ps[:, T_BANK + idx(n) % 2, 0:blocks * P].rearrange("p (k q) -> p k q", q=P)
                        o, hi = (m["pT"][k][:, n % 2, 4 * half:4 * half + blocks, qt * P:qt * P + P] for k in (1, 0))
                        nc.vector.tensor_tensor(o, bank, hi, ALU.subtract).then_inc(t_lo, 1)

                def scores(n, it, qt):
                    w = P * (qt + 1) if L.causal else L.kv
                    dve.wait_ge(s_mm, at(lambda n: c["s"] + QT * n + qt + 1, n, it))
                    dve.nop(nofuse=True)
                    bank = ps[:, S_BANK + 2 * (qt % 2):S_BANK + 2 * (qt % 2) + L.halves, :].rearrange("p a n -> p (a n)")[:, 0:w]
                    kw = dict(out=m["p"][:, qt % 2, 0:w], in0=bank, scalar=3.0e38, op1=ALU.min, accum_out=nb[:, qt % 2:qt % 2 + 1])
                    if L.causal:
                        ins = nc.vector.tensor_tensor_reduce(in1=causal_bias[:, 512 - w:512], scale=-ISQ, op0=ALU.add, **kw)
                    elif L.masked:
                        ins = nc.vector.tensor_tensor_reduce(in1=m["mb"][:, L.batch(n), :], scale=-ISQ, op0=ALU.add, **kw)
                    else:
                        if qt == 0:
                            dve.wait_ge(k_norm, at(lambda n: n + 1, n, it))
                            dve.wait_ge(q_norm, at(lambda n: n + 1, n, it))
                            dve.nop(nofuse=True)
                        kw.update(scalar=-3.0e38, op1=ALU.max, accum_out=m["mx"][:, qt % 2:qt % 2 + 1])
                        nc.vector.tensor_tensor_reduce(in1=m["rk"][:, n % 2, :], scale=m["nq"][:, n % 2, qt:qt + 1], op0=ALU.mult, **kw).then_inc(row_max, 1)
                        dve.wait_ge(row_max, at(lambda n: QT * n + qt + 1, n, it))
                        ins = nc.vector.tensor_scalar(nb[:, qt % 2:qt % 2 + 1], m["mx"][:, qt % 2:qt % 2 + 1], -1.0, None, ALU.mult)
                    ins.then_inc(s_max, 1)

                def unit(n, it):
                    for qt in range(QT):
                        scores(n, it, qt)
                        dve.wait_ge(p_exp, at(lambda n: c["s"] + QT * n + qt + 1, n, it))
                        nc.vector.reciprocal(ri[:, qt % 2:qt % 2 + 1], rs[:, qt % 2:qt % 2 + 1]).then_inc(r_inv, 1)
                        job_parts(n, it, qt, L.jobs(n, qt))
                        if L.rope and qt > 0:
                            rotated(n, it, qt - 1, L.jobs(n, qt - 1))
                        if qt > 0:
                            turned(n, it, qt - 1)
                        elif n > 0:
                            turned(n - 1, it, QT - 1)

                if L.rope:
                    dve.wait_ge(const_in, 32)
                    dve.wait_ge(const_ok, 2)
                if L.rms:
                    dve.wait_ge(const_ok, 5)
                if L.masked:
                    dve.wait_ge(const_in, 64)
                    nc.vector.tensor_reduce(m["any"][:, :], m["m8"][:, :, :], AX.X, ALU.max).then_inc(const_ok, 1)
                    dve.wait_ge(const_ok, 7)
                for qt in range(QT):
                    job_parts(-1, None, qt, L.jobs(-1, qt))
                    if L.rope:
                        rotated(-1, None, qt, L.jobs(-1, qt))
                units(dve, unit)
                turned(UNITS - 1, None, QT - 1)
                for qt in range(QT):
                    job_parts(UNITS, None, qt, L.jobs(UNITS, qt))

                last_attention = names[li + 1:li + 2] == ["ffn1"]
                if last_attention:
                    quantise(0)
                    for k in range(AHEAD):
                        round_gu(k)
                for k in range(NT + 3):
                    if last_attention and AHEAD + k < GU:
                        round_gu(AHEAD + k)
                    if k < NT:
                        residual(k)
                    if 0 <= k - 1 < NT:
                        normalise(k - 1)
                    if 0 <= k - 3 < NT and not last_attention:
                        x_part(NT * (li + 1) + k - 3, k - 3, k - 3)

        @block.tensor
        def _(pe):
            def three(o, l, r, first, last):
                nc.tensor.matmul(o, l(0), r(0), start=first, stop=False)
                nc.tensor.matmul(o, l(0), r(1), start=False, stop=False)
                return nc.tensor.matmul(o, l(1), r(0), start=False, stop=last)

            def turn_x(t, bank):
                for ch in range(XC):
                    last = nc.tensor.transpose(ps[:, bank, ch * P:ch * P + P], xf[:, t, ch * P:ch * P + P], ident[:, :])
                last.then_inc(x_mm, 1)

            pe.wait_ge(const_ok, 4)
            pe.wait_ge(x_in, 16)
            for t in range(NT):
                turn_x(t, t)
            for li, L in enumerate(stages):
                c, m = ledger[li], mem[li]
                if names[li] == "ffn0":
                    pe.wait_ge(x_lo, c["ln"] + NT)
                    n = TOK // E
                    for e in range(E + 2):
                        if e < E:
                            pe.wait_ge(gate_lo, e + 1)
                            pe.wait_ge(up_lo, e + 1)
                            for i in range(4):
                                if e:
                                    pe.wait_ge(prod_ok, 4 * (e - 1) + i + 1)
                                for part in range(2):
                                    for ch in range(XC):
                                        o = part * FFN_I + i * P
                                        last = three(ps[:, i, part * n:part * n + n], lambda k: m["gu"][k][:, e % 2, ch, o:o + P],
                                                     lambda k: xT[k][:, ch, e:TOK:E], ch == 0, ch == XC - 1)
                                last.then_inc(gu_mm, 1)
                        if e >= 2:
                            for k in (2 * e - 4, 2 * e - 3):
                                pe.wait_ge(ln_x, c["ln"] + k + 1)
                                turn_x(*tiles("ffn0")[k])
                        if 1 <= e <= E:
                            pe.wait_ge(inter_lo, e)
                            pe.wait_ge(d_lo, e)
                            if e >= 3:
                                pe.wait_ge(x_lo, NT + c["ln"] + 2 * (e - 2))
                            for b in range(B):
                                bank = tiles("ffn0")[2 * e - 2 + b][1]
                                for i in range(4):
                                    last = three(ps[:, bank, :], lambda k: m["in"][k][:, (e - 1) % 2, i, b * P:b * P + P], lambda k: m["d"][k][:, (e - 1) % 2, i, :], i == 0, i == 3)
                                last.then_inc(y_mm, 1)
                    continue
                if names[li] == "ffn1":
                    def turn_q(k):
                        kind, t = QJ[k]
                        pe.wait_ge(q_ok, k + 1)
                        banks = [6, 7] if k >= GU else [6 + k % 2]
                        if k >= GU:
                            pe.wait_ge(q_T, k)
                        elif k >= 2:
                            pe.wait_ge(q_T, k - 1)
                        if k >= GU and "gud".count(QJ[k - 1][0]):
                            pe.wait_ge(diag_cp, weights_before(k))
                        if kind == "t" and t:
                            pe.wait_ge(fy_ok, t)
                        for blk in range(width(kind) // P):
                            bank = ps[:, banks[blk // 8], :].bitcast(BF16)
                            last = nc.tensor.transpose(bank[:, blk % 8 * P:blk % 8 * P + P], quant_buffers(k)[2][:, blk * P:blk * P + P], idb[:, :])
                        last.then_inc(q_mm, 1)
                        if kind in "gud":
                            w = weights_before(k)
                            pe.wait_ge(diag_ok, w + 1)
                            if kind != "d" and w >= 2:
                                pe.wait_ge(diag_cp, w - 1)
                            bank = ps[:, 7, 3 * P:4 * P] if kind == "d" else ps[:, 4 + k % 2, 0:P]
                            nc.tensor.matmul(bank, ones[:, :], diag(k), start=True, stop=True).then_inc(diag_mm, 1)

                    pe.wait_ge(idb_ok, 1)
                    pe.wait_ge(ln_var, c["ln"])
                    for k in range(GU):
                        turn_q(k)
                    pe.wait_ge(diag_cp, GU)

                    def product(part, t):
                        pe.wait_ge(q_T, QN[("x", t)] + 1)
                        if t:
                            pe.wait_ge(row_y if part else g_ok, t)
                        for n, (lo, hi) in enumerate(CH):
                            for ch in range(XC):
                                last = nc.tensor.matmul(ps[:, 3 * part + n, 0:hi - lo], m["qxT"][:, t % 2, ch, :], m["wT"][:, part * XC + ch, lo:hi], start=ch == 0, stop=ch == XC - 1)
                        last.then_inc(fu_mm if part else fg_mm, 1)

                    turn_q(QN[("x", 0)])
                    turn_q(QN[("x", 1)])
                    product(0, 0)
                    product(1, 0)
                    turn_q(QN[("d", 0)])
                    turn_q(QN[("d", 1)])
                    product(0, 1)
                    turn_q(QN[("d", 2)])
                    turn_q(QN[("d", 3)])
                    for t in range(NT):
                        if t + 2 < NT:
                            turn_q(QN[("x", t + 2)])
                            product(0, t + 2)
                        if t + 1 < NT:
                            product(1, t + 1)
                        turn_q(QN[("t", t)])
                        pe.wait_ge(q_T, QN[("t", t)] + 1)
                        for i in range(IT):
                            last = nc.tensor.matmul(ps[:, 7, :], m["qtT"][:, t % 2, i, :], m["wdT"][:, i, :], start=i == 0, stop=i == IT - 1)
                        last.then_inc(y_mm, 1)
                    continue
                src = xT if L.chunks == XC else cT

                def job(n, it, qt, x, kind, half):
                    b, u = L.batch(n + 1), n + 1
                    bank = ps[:, M_BANK + (L.before(n, qt) + x) % 2, :]
                    pe.wait_ge(job_lo, at(lambda n: c["lo"] + L.before(n, qt) + x - 1, n, it))
                    if kind in ("Q", "K", "V"):
                        pe.wait_ge(w_split, at(lambda n: c["split"] + L.head(n + 1) + 1, n, it))
                    j = L.head(u) % 2
                    w = lambda part, seg, ch: wkv[part][:, j if not L.gqa else 0, (seg * L.chunks + ch) * HD:(seg * L.chunks + ch + 1) * HD]
                    span = S if L.chunks == XC else SC
                    if kind == "Q":
                        for ch in range(XC):
                            last = three(bank, lambda k: wq[k][:, j, ch, :], lambda k: xT[k][:, ch, b * S:(b + 1) * S], ch == 0, ch == XC - 1)
                    elif kind == "K":
                        o = b * span + half * 512
                        for ch in range(L.chunks):
                            last = three(bank, lambda k: w(k, 0, ch), lambda k: src[k][:, ch, o:o + 512], ch == 0, ch == L.chunks - 1)
                    elif kind == "V":
                        for t in range(4):
                            o = b * span + half * 512 + t * P
                            for ch in range(L.chunks):
                                last = three(bank[:, t * P:t * P + P], lambda k: src[k][:, ch, o:o + P], lambda k: w(k, 1, ch), ch == 0, ch == L.chunks - 1)
                    elif kind == "KN":
                        pe.wait_ge(sq_ok, at(lambda n: c["sq"] + 3 * (n + 1) + half + 1, n, it))
                        last = nc.tensor.matmul(bank, ones[:, :], m["sq"][:, :], start=True, stop=True)
                    elif kind == "QN":
                        pe.wait_ge(sq_ok, at(lambda n: c["sq"] + 3 * (n + 1) + 3, n, it))
                        for q in range(QT):
                            last = nc.tensor.matmul(bank[:, q:q + 1], m["sq"][:, q * P:q * P + P], ones[:, 0:1], start=True, stop=True)
                    else:
                        v, pT = L.kvslot(n - 1), (n - 1) % 2
                        pe.wait_ge(t_lo, at(lambda n: CREDIT + c["x"] + QT * n * L.halves, n, it))
                        for kt in range(L.kt):
                            q0 = kt * P if L.causal else 0
                            last = three(bank[:, q0:S], lambda k: m["v"][k][:, v, kt, :], lambda k: m["pT"][k][:, pT, kt, q0:S], kt == 0, kt == L.kt - 1)
                    last.then_inc(job_mm, 1)

                def turn(n, it, qt):
                    pe.wait_ge(p_norm, at(lambda n: c["s"] + QT * n + qt + 1, n, it))
                    for half in range(L.halves):
                        idx = lambda n: c["x"] + (QT * n + qt) * L.halves + half
                        pe.wait_ge(t_lo, at(lambda n: CREDIT + idx(n) - 1, n, it))
                        for k in range(qt + 1 if L.causal else 4):
                            kk = (4 * half + k) * P
                            last = nc.tensor.transpose(ps[:, T_BANK + idx(n) % 2, k * P:k * P + P], m["p"][:, qt % 2, kk:kk + P], ident[:, :])
                        last.then_inc(t_mm, 1)

                def unit(n, it):
                    for qt in range(QT):
                        if qt == 0:
                            pe.wait_ge(job_lo, at(lambda n: c["lo"] + L.before(n - 1, QT - 1), n, it))
                            if L.rope:
                                pe.wait_ge(rope_lo, at(lambda n: c["rope"] + 2 * (n + 1), n, it))
                        pe.wait_ge(s_max, at(lambda n: CREDIT + c["s"] + QT * n + qt - 1, n, it))
                        for half in range(L.halves):
                            w = P * (qt + 1) if L.causal else 512
                            last = three(ps[:, S_BANK + 2 * (qt % 2) + half, 0:w], lambda k: m["q"][k][:, n % 2, qt * P:qt * P + P],
                                         lambda k: m["k"][k][:, L.kvslot(n), half * 512:half * 512 + w], True, True)
                        last.then_inc(s_mm, 1)
                        for x, (kind, half) in enumerate(L.jobs(n, qt)):
                            job(n, it, qt, x, kind, half)
                        if qt > 0:
                            turn(n, it, qt - 1)
                        elif n > 0:
                            turn(n - 1, it, QT - 1)

                pe.wait_ge(x_lo, c["ln"] + NT)
                for qt in range(QT):
                    for x, (kind, half) in enumerate(L.jobs(-1, qt)):
                        job(-1, None, qt, x, kind, half)
                units(pe, unit)
                turn(UNITS - 1, None, QT - 1)
                for qt in range(QT):
                    for x, (kind, half) in enumerate(L.jobs(UNITS, qt)):
                        job(UNITS, None, qt, x, kind, half)

                pe.wait_ge(job_lo, c["lo"] + L.before(UNITS + 1))
                def project(t, h, first, last):
                    b, e = t // 4, t % 4
                    cols = slice(b * S + e, (b + 1) * S, 4)
                    return three(ps[:, t, :], lambda k: oT[k][:, h, cols], lambda k: m["pT"][k][:, h // 8, h % 8, :], first, last)
                for h in range(8):
                    pe.wait_ge(w_split, c["split"] + H + h + 1)
                    for t in range(NT):
                        project(t, h, h == 0, False)
                pe.wait_ge(w_split, c["split"] + 2 * H)
                for t in range(NT + 2):
                    if t < NT:
                        for h in range(8, H):
                            last = project(t, h, False, h == H - 1)
                        last.then_inc(y_mm, 1)
                    if t >= 2 and names[li + 1:li + 2] != ["ffn1"]:
                        pe.wait_ge(ln_x, c["ln"] + t - 1)
                        turn_x(t - 2, t - 2)


def kernel(**inputs):
    import numpy as _np
    import concourse.bacc as _bacc
    from concourse import mybir as _mybir
    from concourse.bass_utils import run_bass_kernel_spmd as _run

    def heads(w, chunks, perm=None):
        w = _np.asarray(w).reshape(chunks, P, -1, HD)
        if perm is not None:
            w = w[..., perm]
        return w.transpose(2, 1, 0, 3)

    def kv(k, v):
        k = _np.concatenate([k, v], axis=2)
        return k.reshape(k.shape[0], P, -1)

    flat = lambda q: q.reshape(q.shape[0], P, -1)
    i = {k: _np.asarray(v) for k, v in inputs.items()}
    perm = _np.concatenate([_np.arange(0, HD, 2), _np.arange(1, HD, 2)])
    freq = 1.0 / 10000.0 ** (_np.arange(0, HD, 2, dtype=_np.float32) / HD)
    ang = _np.outer(freq, _np.arange(S, dtype=_np.float32)).astype(_np.float32)
    arrays = {
        "x": i["x"],
        "ctxT": i["ctx_1024"].reshape(B, SC, CC, P).transpose(3, 0, 2, 1).reshape(P, B * CC, SC),
        "gqk": _np.stack([i["L0_xattn_gq"], i["L0_xattn_gk"]], axis=1),
        "cos": _np.concatenate([_np.cos(ang), _np.cos(ang)]),
        "sin": _np.concatenate([-_np.sin(ang), _np.sin(ang)]),
        "mask": i["mask_BxS2_bf1"].view(_np.uint8),
        "wqself0": flat(heads(i["L0_attn_Wq"], XC, perm)),
        "wkvself0": kv(heads(i["L0_attn_Wk"], XC, perm), heads(i["L0_attn_Wv"], XC)),
        "woself0": i["L0_attn_Wo"].reshape(H, P, D),
        "wqcross0": flat(heads(i["L0_xattn_Wq"], XC)),
        "wkvcross0": kv(heads(i["L0_xattn_Wk"], CC), heads(i["L0_xattn_Wv"], CC)),
        "wocross0": i["L0_xattn_Wo"].reshape(H, P, D),
        "wqself1": flat(heads(i["L1_attn_W_Q"].reshape(H * HD, D).T, XC)),
        "wkvself1": kv(heads(i["L1_attn_W_K"].reshape(H * HD, D).T, XC), heads(i["L1_attn_W_V"].reshape(H * HD, D).T, XC)),
        "woself1": i["L1_attn_W_O"].T.reshape(H, P, D),
        "wqcross1": flat(heads(i["L1_xattn_Wq"], XC)),
        "wkvcross1": kv(heads(i["L1_xattn_Wk"], CC), heads(i["L1_xattn_Wv"], CC)),
        "wocross1": i["L1_xattn_Wo"].reshape(H, P, D),
    }
    arrays["gu"] = i["L0_ffn_gate_up_proj"].reshape(E, XC, P, 2 * FFN_I).transpose(0, 2, 1, 3)
    arrays["down"] = i["L0_ffn_down_proj"].reshape(E, FFN_I // P, P, D).transpose(0, 2, 1, 3)
    arrays["wgate"], arrays["wup"], arrays["wdown"] = i["L1_ffn_w_gate"], i["L1_ffn_w_up"], i["L1_ffn_w_down"]
    arrays["didx"] = i["L1_ffn_down_reorder_index"].reshape(IT, P).T
    nc = _bacc.Bacc("TRN2", target_bir_lowering=False, num_devices=1, dynamic_dma_scratch_size=4096)
    arrays = {f"in_{k}": _np.ascontiguousarray(v) for k, v in arrays.items()}
    args = {k[3:]: nc.dram_tensor(k, v.shape, _mybir.dt.from_np(v.dtype), kind="ExternalInput").ap() for k, v in arrays.items()}
    o = nc.dram_tensor("out_0", (B, S, D), _mybir.dt.float32, kind="ExternalOutput").ap()
    build(nc, args, o)
    r = _run(nc, [arrays], core_ids=[0])
    return r.results[0]["out_0"]
```
